# Optimizing a Trainium2 kernel written in Bass

```python
import numpy as np
import jax
import jax.numpy as jnp

def _softmax(x, axis=-1):
    return jax.nn.softmax(x, axis=axis)

def _gelu(x):
    return jax.nn.gelu(x, approximate=True)

def _silu(x):
    return jax.nn.silu(x)

def _sigmoid(x):
    return jax.nn.sigmoid(x)

def _layernorm(x, axis=-1, eps=1e-05):
    m = jnp.mean(x, axis=axis, keepdims=True)
    v = jnp.var(x, axis=axis, keepdims=True)
    return (x - m) / jnp.sqrt(v + eps)

def _scatter_add(tgt, idx, src, axis=0):
    return tgt.at[idx].add(src)

def _segment_sum(src, seg, n):
    return jax.ops.segment_sum(src, seg, n)
kernel_name = 'mk_dlrm_tower_d1_rec_r8_3ad142'

def setup_inputs(seed: int=0):
    np.random.seed(seed)
    _w = jnp.asarray

    def _rec_inputs():
        import jax
        import jax.numpy as jnp
        _tk = jax.random.key(seed)
        dense_ctx = jax.random.normal(jax.random.fold_in(_tk, 190), (512, 16), jnp.float32)
        ids = jnp.stack([jax.random.randint(jax.random.fold_in(_tk, 200 + f), (512,), 0, v, jnp.int32) for f, v in enumerate([12500, 1250, 1250, 1250, 12500, 1000, 12500, 12500, 1000, 1000, 125000, 12500, 1250, 1250, 1250, 1000, 1250, 12500, 12500, 1000, 1250, 12500, 1250, 1000, 12500, 125000, 125000, 125000, 1000, 1250, 1250, 12500, 1000, 12500, 1000, 125000, 1000, 125000, 12500])], axis=1)
        tbl_0 = 0.05 * jax.random.normal(jax.random.fold_in(_tk, 500 + 0), (12500, 16), jnp.float32)
        tbl_1 = 0.05 * jax.random.normal(jax.random.fold_in(_tk, 500 + 1), (1250, 16), jnp.float32)
        tbl_2 = 0.05 * jax.random.normal(jax.random.fold_in(_tk, 500 + 2), (1250, 16), jnp.float32)
        tbl_3 = 0.05 * jax.random.normal(jax.random.fold_in(_tk, 500 + 3), (1250, 16), jnp.float32)
        tbl_4 = 0.05 * jax.random.normal(jax.random.fold_in(_tk, 500 + 4), (12500, 16), jnp.float32)
        tbl_5 = 0.05 * jax.random.normal(jax.random.fold_in(_tk, 500 + 5), (1000, 16), jnp.float32)
        tbl_6 = 0.05 * jax.random.normal(jax.random.fold_in(_tk, 500 + 6), (12500, 16), jnp.float32)
        tbl_7 = 0.05 * jax.random.normal(jax.random.fold_in(_tk, 500 + 7), (12500, 16), jnp.float32)
        tbl_8 = 0.05 * jax.random.normal(jax.random.fold_in(_tk, 500 + 8), (1000, 16), jnp.float32)
        tbl_9 = 0.05 * jax.random.normal(jax.random.fold_in(_tk, 500 + 9), (1000, 16), jnp.float32)
        tbl_10 = 0.05 * jax.random.normal(jax.random.fold_in(_tk, 500 + 10), (125000, 16), jnp.float32)
        tbl_11 = 0.05 * jax.random.normal(jax.random.fold_in(_tk, 500 + 11), (12500, 16), jnp.float32)
        tbl_12 = 0.05 * jax.random.normal(jax.random.fold_in(_tk, 500 + 12), (1250, 16), jnp.float32)
        tbl_13 = 0.05 * jax.random.normal(jax.random.fold_in(_tk, 500 + 13), (1250, 16), jnp.float32)
        tbl_14 = 0.05 * jax.random.normal(jax.random.fold_in(_tk, 500 + 14), (1250, 16), jnp.float32)
        tbl_15 = 0.05 * jax.random.normal(jax.random.fold_in(_tk, 500 + 15), (1000, 16), jnp.float32)
        tbl_16 = 0.05 * jax.random.normal(jax.random.fold_in(_tk, 500 + 16), (1250, 16), jnp.float32)
        tbl_17 = 0.05 * jax.random.normal(jax.random.fold_in(_tk, 500 + 17), (12500, 16), jnp.float32)
        tbl_18 = 0.05 * jax.random.normal(jax.random.fold_in(_tk, 500 + 18), (12500, 16), jnp.float32)
        tbl_19 = 0.05 * jax.random.normal(jax.random.fold_in(_tk, 500 + 19), (1000, 16), jnp.float32)
        tbl_20 = 0.05 * jax.random.normal(jax.random.fold_in(_tk, 500 + 20), (1250, 16), jnp.float32)
        tbl_21 = 0.05 * jax.random.normal(jax.random.fold_in(_tk, 500 + 21), (12500, 16), jnp.float32)
        tbl_22 = 0.05 * jax.random.normal(jax.random.fold_in(_tk, 500 + 22), (1250, 16), jnp.float32)
        tbl_23 = 0.05 * jax.random.normal(jax.random.fold_in(_tk, 500 + 23), (1000, 16), jnp.float32)
        tbl_24 = 0.05 * jax.random.normal(jax.random.fold_in(_tk, 500 + 24), (12500, 16), jnp.float32)
        tbl_25 = 0.05 * jax.random.normal(jax.random.fold_in(_tk, 500 + 25), (125000, 16), jnp.float32)
        tbl_26 = 0.05 * jax.random.normal(jax.random.fold_in(_tk, 500 + 26), (125000, 16), jnp.float32)
        tbl_27 = 0.05 * jax.random.normal(jax.random.fold_in(_tk, 500 + 27), (125000, 16), jnp.float32)
        tbl_28 = 0.05 * jax.random.normal(jax.random.fold_in(_tk, 500 + 28), (1000, 16), jnp.float32)
        tbl_29 = 0.05 * jax.random.normal(jax.random.fold_in(_tk, 500 + 29), (1250, 16), jnp.float32)
        tbl_30 = 0.05 * jax.random.normal(jax.random.fold_in(_tk, 500 + 30), (1250, 16), jnp.float32)
        tbl_31 = 0.05 * jax.random.normal(jax.random.fold_in(_tk, 500 + 31), (12500, 16), jnp.float32)
        tbl_32 = 0.05 * jax.random.normal(jax.random.fold_in(_tk, 500 + 32), (1000, 16), jnp.float32)
        tbl_33 = 0.05 * jax.random.normal(jax.random.fold_in(_tk, 500 + 33), (12500, 16), jnp.float32)
        tbl_34 = 0.05 * jax.random.normal(jax.random.fold_in(_tk, 500 + 34), (1000, 16), jnp.float32)
        tbl_35 = 0.05 * jax.random.normal(jax.random.fold_in(_tk, 500 + 35), (125000, 16), jnp.float32)
        tbl_36 = 0.05 * jax.random.normal(jax.random.fold_in(_tk, 500 + 36), (1000, 16), jnp.float32)
        tbl_37 = 0.05 * jax.random.normal(jax.random.fold_in(_tk, 500 + 37), (125000, 16), jnp.float32)
        tbl_38 = 0.05 * jax.random.normal(jax.random.fold_in(_tk, 500 + 38), (12500, 16), jnp.float32)
        _rk = jax.random.fold_in(_tk, 7)
        W_top1 = 0.0606339 * jax.random.normal(jax.random.fold_in(_tk, 801), (272, 512), jnp.float32)
        W_top2 = 0.0441942 * jax.random.normal(jax.random.fold_in(_tk, 802), (512, 256), jnp.float32)
        W_top3 = 0.0625 * jax.random.normal(jax.random.fold_in(_tk, 803), (256, 1), jnp.float32)
        b_top1 = jnp.zeros((512,), jnp.float32)
        b_top2 = jnp.zeros((256,), jnp.float32)
        return (dense_ctx, ids, tbl_0, tbl_1, tbl_2, tbl_3, tbl_4, tbl_5, tbl_6, tbl_7, tbl_8, tbl_9, tbl_10, tbl_11, tbl_12, tbl_13, tbl_14, tbl_15, tbl_16, tbl_17, tbl_18, tbl_19, tbl_20, tbl_21, tbl_22, tbl_23, tbl_24, tbl_25, tbl_26, tbl_27, tbl_28, tbl_29, tbl_30, tbl_31, tbl_32, tbl_33, tbl_34, tbl_35, tbl_36, tbl_37, tbl_38, W_top1, b_top1, W_top2, b_top2, W_top3)
    dense_ctx, ids, tbl_0, tbl_1, tbl_2, tbl_3, tbl_4, tbl_5, tbl_6, tbl_7, tbl_8, tbl_9, tbl_10, tbl_11, tbl_12, tbl_13, tbl_14, tbl_15, tbl_16, tbl_17, tbl_18, tbl_19, tbl_20, tbl_21, tbl_22, tbl_23, tbl_24, tbl_25, tbl_26, tbl_27, tbl_28, tbl_29, tbl_30, tbl_31, tbl_32, tbl_33, tbl_34, tbl_35, tbl_36, tbl_37, tbl_38, W_top1, b_top1, W_top2, b_top2, W_top3 = _rec_inputs()

    def _L0_rec_setup():
        import jax, jax.numpy as jnp
        import numpy as np
        B, F0, D = (256, 39, 16)
        H1, H2 = (128, 128)
        key = jax.random.key(seed)
        k1, k2, k3 = jax.random.split(key, 3)
        x = jax.random.normal(k1, (B, F0, D), dtype=jnp.float32)

        def xavier(k, out_c, in_c):
            bound = np.sqrt(6.0 / (in_c + out_c)).astype(np.float32)
            return jax.random.uniform(k, (out_c, in_c, 1), dtype=jnp.float32, minval=-bound, maxval=bound)
        W0 = xavier(k2, H1, F0 * F0)
        W1 = xavier(k3, H2, F0 * H1)
        return {'input': x, 'W0': W0, 'W1': W1}
    _L0_rec_all = _L0_rec_setup()
    _L0_rec_in = {k: v for k, v in _L0_rec_all.items() if k in ('W0', 'W1')}
    del _L0_rec_all
    return {'dense_ctx': dense_ctx, 'ids': ids, 'tbl_0': tbl_0, 'tbl_1': tbl_1, 'tbl_2': tbl_2, 'tbl_3': tbl_3, 'tbl_4': tbl_4, 'tbl_5': tbl_5, 'tbl_6': tbl_6, 'tbl_7': tbl_7, 'tbl_8': tbl_8, 'tbl_9': tbl_9, 'tbl_10': tbl_10, 'tbl_11': tbl_11, 'tbl_12': tbl_12, 'tbl_13': tbl_13, 'tbl_14': tbl_14, 'tbl_15': tbl_15, 'tbl_16': tbl_16, 'tbl_17': tbl_17, 'tbl_18': tbl_18, 'tbl_19': tbl_19, 'tbl_20': tbl_20, 'tbl_21': tbl_21, 'tbl_22': tbl_22, 'tbl_23': tbl_23, 'tbl_24': tbl_24, 'tbl_25': tbl_25, 'tbl_26': tbl_26, 'tbl_27': tbl_27, 'tbl_28': tbl_28, 'tbl_29': tbl_29, 'tbl_30': tbl_30, 'tbl_31': tbl_31, 'tbl_32': tbl_32, 'tbl_33': tbl_33, 'tbl_34': tbl_34, 'tbl_35': tbl_35, 'tbl_36': tbl_36, 'tbl_37': tbl_37, 'tbl_38': tbl_38, 'W_top1': W_top1, 'b_top1': b_top1, 'W_top2': W_top2, 'b_top2': b_top2, 'W_top3': W_top3, 'L0_rec_W0': _L0_rec_in['W0'], 'L0_rec_W1': _L0_rec_in['W1']}

def reference(dense_ctx, ids, tbl_0, tbl_1, tbl_2, tbl_3, tbl_4, tbl_5, tbl_6, tbl_7, tbl_8, tbl_9, tbl_10, tbl_11, tbl_12, tbl_13, tbl_14, tbl_15, tbl_16, tbl_17, tbl_18, tbl_19, tbl_20, tbl_21, tbl_22, tbl_23, tbl_24, tbl_25, tbl_26, tbl_27, tbl_28, tbl_29, tbl_30, tbl_31, tbl_32, tbl_33, tbl_34, tbl_35, tbl_36, tbl_37, tbl_38, W_top1, b_top1, W_top2, b_top2, W_top3, L0_rec_W0, L0_rec_W1):
    import jax
    import jax.numpy as jnp

    def _L0_rec_ref(input, W0, W1):
        import jax, jax.numpy as jnp
        import numpy as np
        B, F0, D = (256, 39, 16)
        H1, H2 = (128, 128)
        x0 = input
        h = input
        outs = []
        for W in (W0, W1):
            Hout, P, _ = W.shape
            Hk = h.shape[1]
            Wr = W[:, :, 0].reshape(Hout, x0.shape[1], Hk)
            h = jnp.einsum('bfd,bqd,hfq->bhd', x0, h, Wr)
            outs.append(h)
        result = jnp.concatenate(outs, axis=1)
        return jnp.sum(result, axis=2)
    e = jnp.stack([tbl_0[ids[:, 0]], tbl_1[ids[:, 1]], tbl_2[ids[:, 2]], tbl_3[ids[:, 3]], tbl_4[ids[:, 4]], tbl_5[ids[:, 5]], tbl_6[ids[:, 6]], tbl_7[ids[:, 7]], tbl_8[ids[:, 8]], tbl_9[ids[:, 9]], tbl_10[ids[:, 10]], tbl_11[ids[:, 11]], tbl_12[ids[:, 12]], tbl_13[ids[:, 13]], tbl_14[ids[:, 14]], tbl_15[ids[:, 15]], tbl_16[ids[:, 16]], tbl_17[ids[:, 17]], tbl_18[ids[:, 18]], tbl_19[ids[:, 19]], tbl_20[ids[:, 20]], tbl_21[ids[:, 21]], tbl_22[ids[:, 22]], tbl_23[ids[:, 23]], tbl_24[ids[:, 24]], tbl_25[ids[:, 25]], tbl_26[ids[:, 26]], tbl_27[ids[:, 27]], tbl_28[ids[:, 28]], tbl_29[ids[:, 29]], tbl_30[ids[:, 30]], tbl_31[ids[:, 31]], tbl_32[ids[:, 32]], tbl_33[ids[:, 33]], tbl_34[ids[:, 34]], tbl_35[ids[:, 35]], tbl_36[ids[:, 36]], tbl_37[ids[:, 37]], tbl_38[ids[:, 38]]], axis=1)
    z = _L0_rec_ref(e, L0_rec_W0, L0_rec_W1)
    z = z.reshape(z.shape[0], -1)
    h = jnp.concatenate([z, dense_ctx], axis=1)
    h = jnp.maximum(h @ W_top1 + b_top1, 0.0)
    h = jnp.maximum(h @ W_top2 + b_top2, 0.0)
    y = h @ W_top3
    return y

_drawn_inputs = setup_inputs


def setup_inputs(seed=0):
    import zlib

    import numpy as np

    out = dict(_drawn_inputs(seed))
    spreads = {'b_top1': (0.0, 0.1), 'b_top2': (0.0, 0.1)}
    factors = {'tbl_0': 6.811,
     'tbl_1': 6.339,
     'tbl_2': 6.936,
     'tbl_3': 6.997,
     'tbl_4': 7.158,
     'tbl_5': 7.419,
     'tbl_6': 7.14,
     'tbl_7': 6.802,
     'tbl_8': 7.506,
     'tbl_9': 7.294,
     'tbl_10': 7.485,
     'tbl_11': 6.758,
     'tbl_12': 7.351,
     'tbl_13': 7.32,
     'tbl_14': 7.467,
     'tbl_15': 6.84,
     'tbl_16': 6.471,
     'tbl_17': 7.84,
     'tbl_18': 7.454,
     'tbl_19': 7.258,
     'tbl_20': 6.94,
     'tbl_21': 7.46,
     'tbl_22': 7.398,
     'tbl_23': 7.227,
     'tbl_24': 6.363,
     'tbl_25': 7.055,
     'tbl_26': 7.067,
     'tbl_27': 6.992,
     'tbl_28': 7.308,
     'tbl_29': 7.238,
     'tbl_30': 6.669,
     'tbl_31': 6.927,
     'tbl_32': 7.16,
     'tbl_33': 6.827,
     'tbl_34': 7.499,
     'tbl_35': 7.608,
     'tbl_36': 7.305,
     'tbl_37': 6.441,
     'tbl_38': 6.579,
     'L0_rec_W1': 8.0}
    for name, (base, spread) in spreads.items():
        noise = np.random.default_rng([zlib.crc32(name.encode()), seed]).standard_normal(out[name].shape)
        drawn = base * np.exp(spread * noise) if base else spread * noise
        out[name] = jnp.asarray(drawn.astype(out[name].dtype))
    for name, factor in factors.items():
        out[name] = (out[name] * factor).astype(out[name].dtype)
    return out
```

```python
from contextlib import ExitStack

import numpy as np

import concourse.bass as bass
from concourse import mybir

F32 = mybir.dt.float32
F32R = mybir.dt.float32r
I32 = mybir.dt.int32
U32 = mybir.dt.uint32
ALU = mybir.AluOpType
ACT = mybir.ActivationFunctionType

P = 128
BATCH = 512
FIELDS = 39
DIM = 16
HID = 128
DENSE = 16
TOP1 = 512
TOP2 = 256
BTILES = BATCH // P

BLOCKS = 3
ROWS = BLOCKS * FIELDS
FANS = 2
PLAIN = tuple(-FANS * BLOCKS * a % FIELDS for a in range(4))
STACKS = FANS + len(PLAIN)
TILES = ((0, 0, 3), (1, 0, 3), (0, 1, 3), (1, 1, 3), (0, 2, 3), (1, 2, 3), (0, 3, 2))
NT = len(TILES)


def covered_differences():
    out = []
    for fan, plain, blocks in TILES:
        for j in range(blocks):
            gap = (fan * BLOCKS + j - PLAIN[plain]) % FIELDS
            out.append(min(gap, FIELDS - gap))
    return sorted(out)


assert covered_differences() == list(range(FIELDS // 2 + 1))

CHUNK_D = 4
CHUNKS = DIM // CHUNK_D
COLS = CHUNK_D * P
STEPS = BTILES * CHUNKS
SLOTS = CHUNKS * NT
GROUP = P // DIM
GROUPS = P // GROUP
XF = FIELDS + 1
PAIRS = (NT + 1) // 2
P_RING = 2
SPLIT_RING = 5

XT_SLOT = (0, 1)
H_SLOT = (2, 8, 12, 16)
G_SLOT = 5
Z2_SLOT = 21
Z2_PARTS = ((0, 8), (8, 16), (16, 24), (24, 32), (32, FIELDS))
MLP1_SLOT = Z2_SLOT + len(Z2_PARTS)
MLP2_SLOT = MLP1_SLOT + 1
assert MLP2_SLOT < SLOTS
WT_BANKS = (FIELDS + 3) // 4


def build(nc, ids, tables, dense, w0, w1, wt1, b1, wt2, b2, wt3, out):
    with ExitStack() as ctx:
        def sb(name, shape, dt=F32):
            return ctx.enter_context(nc.sbuf_tensor(name, shape, dt))

        def bank(name):
            return ctx.enter_context(nc.psum_tensor(name, [P, 512], F32))

        def sem(name):
            return ctx.enter_context(nc.semaphore(name))

        idx = sb("idx", [P, BTILES, FIELDS], I32)
        x_rows = sb("x_rows", [P, 2, FIELDS * DIM])
        x_wide = sb("x_wide", [P, (4 + FANS * BLOCKS) * FIELDS * DIM])
        ident = sb("ident", [P, P])
        stacks = sb("stacks", [P, 2 * P * DIM + 2 * COLS])
        pairs = sb("pairs", [P, P_RING, 2, COLS])
        pairs_hi = sb("pairs_hi", [P, SPLIT_RING, 2, COLS], F32R)
        pairs_lo = sb("pairs_lo", [P, SPLIT_RING, 2, COLS], F32R)
        w0_hi = sb("w0_hi", [P, NT, P], F32R)
        w0_lo = sb("w0_lo", [P, NT, P], F32R)
        w1_t = sb("w1_t", [P, FIELDS, P])
        h1 = sb("h1", [P, 2, P * DIM])
        h1_rows = sb("h1_rows", [P, 2, 4, P])
        x_cols = sb("x_cols", [P, GROUPS, XF])
        x_diag = sb("x_diag", [P, GROUPS, GROUP * XF])
        gram = sb("gram", [P, XF, P])
        z2_sb = sb("z2_sb", [P, P])
        dense_sb = sb("dense_sb", [P, BTILES, DENSE])
        dense_t = sb("dense_t", [DENSE, BATCH])
        wt1_z = sb("wt1_z", [P, 2, TOP1])
        wt1_d = sb("wt1_d", [DENSE, TOP1])
        wt2_sb = sb("wt2_sb", [P, TOP1 // P, TOP2])
        wt3_sb = sb("wt3_sb", [P, TOP2 // P])
        b1_sb = sb("b1_sb", [P, TOP1 // P])
        b2_sb = sb("b2_sb", [P, TOP2 // P])
        hid1 = sb("hid1", [P, TOP1 // P, P])
        hid2 = sb("hid2", [P, TOP2 // P, P])
        y_sb = sb("y_sb", [1, BATCH])

        x_rep = x_wide[:, 0:4 * FIELDS * DIM].rearrange("p (f d) -> p f d", d=DIM)
        x_fan = x_wide[:, 4 * FIELDS * DIM:].rearrange("p (f d) -> p f d", d=DIM)

        def fan0_tile(tile):
            return stacks[:, (tile % 2) * P * DIM:(tile % 2 + 1) * P * DIM]

        def fan_chunk(fan, s, rows):
            if fan == 0:
                c = s % CHUNKS
                by_d = fan0_tile(s // CHUNKS)[0:rows].rearrange("p (b d) -> p d b", d=DIM)
                return by_d[:, c * CHUNK_D:(c + 1) * CHUNK_D, :]
            at = 2 * P * DIM + (s % 2) * COLS
            return stacks[0:rows, at:at + COLS].rearrange("p (d b) -> p d b", b=P)

        wsym = x_wide[:, 0:4 * FIELDS * FIELDS].rearrange("p (f q) -> p f q", q=2 * FIELDS)
        w0_raw = stacks[:, 0:FIELDS * FIELDS].rearrange("p (f q) -> p f q", q=FIELDS)
        w0_tiles = stacks[:, 2048:2048 + NT * ROWS].rearrange("p (n r) -> p n r", r=ROWS)
        w1_raw = gram[:].rearrange("p f q -> p (f q)")[:, 0:FIELDS * HID].rearrange(
            "p (f q) -> p f q", q=HID)

        T = [bank("stack_bank0"), bank("stack_bank1")]
        L = [bank("layer1_bank0"), bank("layer1_bank1")]
        H = bank("h1_rows_bank")
        G = [bank("gram_bank0"), bank("gram_bank1")]
        M = bank("tower_bank")

        ids_in = sem("ids_in")
        w0_in = sem("w0_in")
        w1_in = sem("w1_in")
        small_in = sem("small_in")
        x_landed = [sem(f"x_landed{t}") for t in range(BTILES)]
        ident_zero = sem("ident_zero")
        ident_done = sem("ident_done")
        sym_done = sem("sym_done")
        w0_tiled = sem("w0_tiled")
        consts_done = sem("consts_done")
        w0_turned = sem("w0_turned")
        w0_hi_done = sem("w0_hi_done")
        w0_lo_done = sem("w0_lo_done")
        w1_turned = sem("w1_turned")
        w1_kept_act = sem("w1_kept_act")
        w1_kept_dve = sem("w1_kept_dve")
        dense_turned = sem("dense_turned")
        dense_kept = sem("dense_kept")
        x_rep_done = sem("x_rep_done")
        x_fan_done = sem("x_fan_done")
        stack_turned = sem("stack_turned")
        stack_kept = sem("stack_kept")
        pairs_done = sem("pairs_done")
        hi_done = sem("hi_done")
        lo_done = sem("lo_done")
        tile_used = sem("tile_used")
        h1_kept = sem("h1_kept")
        xcols_turned = sem("xcols_turned")
        xcols_kept = sem("xcols_kept")
        xdiag_in = [sem("xdiag_in0"), sem("xdiag_in1")]
        rows_turned = sem("rows_turned")
        rows_kept = sem("rows_kept")
        gram_done = sem("gram_done")
        gram_kept = sem("gram_kept")
        z2_done = sem("z2_done")
        z2_kept = sem("z2_kept")
        top1_done = sem("top1_done")
        top1_kept = sem("top1_kept")
        top2_done = sem("top2_done")
        top2_kept = sem("top2_kept")
        y_done = sem("y_done")
        y_kept = sem("y_kept")
        y_out = sem("y_out")

        SMALL_LOADS = 7
        W0_PARTS = ((0, 4), (4, NT - 1), (NT - 1, NT))

        def tile_rows(n):
            return TILES[n][2] * FIELDS

        def w0_bank(n0, n1):
            cols = T[n0 // 4][0:tile_rows(n0), (n0 % 4) * HID:(n0 % 4 + n1 - n0) * HID]
            return cols.rearrange("p (n h) -> p n h", h=HID)

        def w1_bank(n):
            return (L + G)[n % 4]

        def w1_count(n):
            return min(4, FIELDS - 4 * n)

        def kept_before(n, parity):
            return (n - parity) // 2 + 1

        def pair_slot(s, pair):
            return (s * PAIRS + pair) % SPLIT_RING

        block = ctx.enter_context(nc.Block())

        @block.sync
        def _(sp):
            sp.dma_start(idx[:], ids).then_inc(ids_in, 16)
            sp.dma_start(w0_raw, w0).then_inc(w0_in, 16)
            sp.dma_start(w1_raw, w1).then_inc(w1_in, 16)
            sp.dma_start(dense_sb[:], dense.rearrange("(t p) c -> p t c", p=P)).then_inc(small_in, 16)
            sp.dma_start(wt1_z[:], wt1[0:2 * HID, :].rearrange("(k p) n -> p k n", p=P)).then_inc(small_in, 16)
            sp.dma_start(wt1_d[:], wt1[2 * HID:2 * HID + DENSE, :]).then_inc(small_in, 16)
            sp.dma_start(wt2_sb[:], wt2.rearrange("(k p) n -> p k n", p=P)).then_inc(small_in, 16)
            sp.dma_start(wt3_sb[:], wt3).then_inc(small_in, 16)
            sp.dma_start(b1_sb[:], b1).then_inc(small_in, 16)
            sp.dma_start(b2_sb[:], b2).then_inc(small_in, 16)
            for u in range(BTILES):
                for half in range(2):
                    g0, g1 = half * GROUPS // 2, (half + 1) * GROUPS // 2
                    sp.wait_ge(xcols_kept, 2 * u + half + 1)
                    if u:
                        sp.wait_ge(gram_done, (u - 1) * GROUPS + g1)
                    else:
                        sp.wait_ge(consts_done, 2)
                    for b in range(GROUP):
                        rows = slice(b * DIM, (b + 1) * DIM)
                        sp.dma_start(x_diag[rows, g0:g1, b * XF:(b + 1) * XF],
                                     x_cols[rows, g0:g1, :]).then_inc(xdiag_in[half], 16)
            sp.wait_ge(y_kept, BTILES)
            sp.dma_start(out, y_sb[:]).then_inc(y_out, 16)
            sp.wait_ge(y_out, 16)

        @block.gpsimd
        def _(pool):
            nc.gpsimd.memset(ident[:], 0.0).then_inc(ident_zero, 1)
            pool.wait_ge(ident_zero, 1)
            nc.gpsimd.affine_select(out=ident[:], in_=ident[:], compare_op=ALU.not_equal, fill=1.0,
                                    base=0, pattern=[[-1, P]], channel_multiplier=1).then_inc(ident_done, 1)
            pool.wait_ge(ids_in, 16)
            for t in range(BTILES):
                if t >= 2:
                    pool.wait_ge(x_rep_done, t - 1)
                for f in range(FIELDS):
                    nc.gpsimd.indirect_dma_start(
                        out=x_rows[:, t % 2, f * DIM:(f + 1) * DIM], out_offset=None, in_=tables[f],
                        in_offset=bass.IndirectOffsetOnAxis(ap=idx[:, t, f:f + 1].bitcast(U32), axis=0),
                    ).then_inc(x_landed[t], 16)

        @block.scalar
        def _(act):
            act.wait_ge(w0_turned, 2)
            for n0, n1 in W0_PARTS:
                nc.scalar.activation(w0_hi[0:tile_rows(n0), n0:n1, :], w0_bank(n0, n1),
                                     ACT.Copy).then_inc(w0_hi_done, 1)
            for n in range(0, WT_BANKS, 2):
                act.wait_ge(w1_turned, n + 1)
                nc.scalar.activation(w1_t[:, 4 * n:4 * n + w1_count(n), :],
                                     w1_bank(n)[:, 0:w1_count(n) * HID].rearrange("p (n h) -> p n h", h=HID),
                                     ACT.Copy).then_inc(w1_kept_act, 1)
            act.wait_ge(dense_turned, 1)
            nc.scalar.activation(dense_t[:], H[0:DENSE, :], ACT.Copy).then_inc(dense_kept, 1)

            def rotate_fields(t, fan):
                act.wait_ge(x_rep_done, t + 1)
                at = x_rep[:, fan * BLOCKS, 0:1]
                rotated = bass.AP(tensor=at.tensor, offset=at.offset,
                                  ap=[list(at.ap[0]), [DIM, BLOCKS], [1, FIELDS * DIM]])
                nc.scalar.activation(
                    x_fan[:, fan * ROWS:(fan + 1) * ROWS, :].rearrange("p (j f) d -> p j (f d)", j=BLOCKS),
                    rotated, ACT.Copy).then_inc(x_fan_done, 1)

            def keep_fan(s, fan):
                act.wait_ge(stack_turned, STACKS * s + fan + 1)
                if s >= 2:
                    act.wait_ge(pairs_done, NT * (s - 1))
                if fan == 0 and s >= 2 * CHUNKS and s % CHUNKS == 0:
                    act.wait_ge(xcols_turned, 2 * (s // CHUNKS - 1))
                nc.scalar.activation(fan_chunk(fan, s, ROWS),
                                     T[fan][0:ROWS, :].rearrange("p (d b) -> p d b", b=P),
                                     ACT.Copy).then_inc(stack_kept, 1)

            def round_pairs(s, pair):
                tiles = min(2, NT - 2 * pair)
                rows = FIELDS * TILES[2 * pair][2]
                at = s * PAIRS + pair
                act.wait_ge(pairs_done, NT * s + 2 * pair + tiles)
                if at >= SPLIT_RING:
                    old = at - SPLIT_RING
                    act.wait_ge(tile_used, NT * (old // PAIRS) + min(2 * (old % PAIRS) + 2, NT))
                nc.scalar.activation(pairs_hi[0:rows, pair_slot(s, pair), 0:tiles, :],
                                     pairs[0:rows, (s * PAIRS + pair) % P_RING, 0:tiles, :],
                                     ACT.Copy).then_inc(hi_done, 1)

            def side(u, k):
                if k in XT_SLOT:
                    half = k - XT_SLOT[0]
                    g0 = half * GROUPS // 2
                    act.wait_ge(xcols_turned, 2 * u + half + 1)
                    if u:
                        act.wait_ge(xdiag_in[half], 16 * GROUP * u)
                    else:
                        act.wait_ge(consts_done, 2)
                    nc.scalar.activation(
                        x_cols[:, g0:g0 + GROUPS // 2, 0:FIELDS],
                        M[:, 0:GROUPS // 2 * FIELDS].rearrange("p (g f) -> p g f", f=FIELDS),
                        ACT.Copy).then_inc(xcols_kept, 1)
                if G_SLOT <= k < G_SLOT + GROUPS:
                    g = k - G_SLOT
                    act.wait_ge(gram_done, u * GROUPS + g + 1)
                    if u and g == 0:
                        act.wait_ge(top1_done, u)
                    nc.scalar.activation(
                        gram[:, :, g * GROUP:(g + 1) * GROUP].rearrange("p f b -> p b f"),
                        G[g % 2][:, 0:GROUP * XF].rearrange("p (b f) -> p b f", f=XF),
                        ACT.Copy).then_inc(gram_kept, 1)
                if k == MLP1_SLOT:
                    act.wait_ge(top1_done, u + 1)
                    if u == 0:
                        act.wait_ge(small_in, 16 * SMALL_LOADS)
                    else:
                        act.wait_ge(top2_done, u)
                    for m in range(TOP1 // P):
                        nc.scalar.activation(hid1[:, m, :], M[:, m * P:(m + 1) * P], ACT.Relu,
                                             bias=b1_sb[:, m:m + 1]).then_inc(top1_kept, 1)
                if k == MLP2_SLOT:
                    act.wait_ge(top2_done, u + 1)
                    if u:
                        act.wait_ge(y_done, u)
                    for m in range(TOP2 // P):
                        nc.scalar.activation(hid2[:, m, :], M[:, m * P:(m + 1) * P], ACT.Relu,
                                             bias=b2_sb[:, m:m + 1]).then_inc(top2_kept, 1)

            for s in range(-1, STEPS + CHUNKS):
                if s + 1 < STEPS and (s + 1) % CHUNKS == 0:
                    rotate_fields((s + 1) // CHUNKS, 0)
                    rotate_fields((s + 1) // CHUNKS, 1)
                for n in range(NT):
                    if s + 1 < STEPS:
                        if n < FANS:
                            keep_fan(s + 1, n)
                        if n >= 3:
                            round_pairs(s + 1, n - 3)
                    if s >= CHUNKS:
                        side(s // CHUNKS - 1, s % CHUNKS * NT + n)

        @block.vector
        def _(dve):
            nc.vector.memset(x_diag[:], 0.0).then_inc(consts_done, 1)
            nc.vector.memset(x_cols[:], 1.0).then_inc(consts_done, 1)
            dve.wait_ge(w0_in, 16)
            corner = wsym[:, 0:FIELDS, 0:FIELDS]
            nc.vector.tensor_tensor(corner, w0_raw, w0_raw.rearrange("p f q -> p q f"), ALU.add).then_inc(sym_done, 1)
            dve.wait_ge(sym_done, 1)
            diagonal = bass.AP(tensor=corner.tensor, offset=corner.offset,
                               ap=[list(corner.ap[0]), [2 * FIELDS + 1, FIELDS]])
            nc.vector.tensor_scalar(diagonal, diagonal, 0.5, None, ALU.mult).then_inc(sym_done, 1)
            dve.wait_ge(sym_done, 2)
            nc.vector.tensor_copy(wsym[:, 0:FIELDS, FIELDS:2 * FIELDS], corner).then_inc(sym_done, 1)
            dve.wait_ge(sym_done, 3)
            nc.vector.tensor_copy(wsym[:, FIELDS:2 * FIELDS, :], wsym[:, 0:FIELDS, :]).then_inc(sym_done, 1)
            for n, (fan, plain, blocks) in enumerate(TILES):
                dve.wait_ge(sym_done, 4)
                at = wsym[:, fan * BLOCKS, PLAIN[plain]:PLAIN[plain] + 1]
                rows = bass.AP(tensor=at.tensor, offset=at.offset,
                               ap=[list(at.ap[0]), [2 * FIELDS, blocks], [2 * FIELDS + 1, FIELDS]])
                nc.vector.tensor_copy(w0_tiles[:, n, 0:blocks * FIELDS].rearrange("p (j f) -> p j f", j=blocks),
                                      rows).then_inc(w0_tiled, 1)
            for i, (n0, n1) in enumerate(W0_PARTS):
                dve.wait_ge(w0_hi_done, 1 if i == 0 else len(W0_PARTS))
                nc.vector.tensor_tensor(w0_lo[0:tile_rows(n0), n0:n1, :], w0_bank(n0, n1),
                                        w0_hi[0:tile_rows(n0), n0:n1, :].bitcast(F32),
                                        ALU.subtract).then_inc(w0_lo_done, 1)
            for n in range(1, WT_BANKS, 2):
                dve.wait_ge(w1_turned, n + 1)
                nc.vector.tensor_copy(w1_t[:, 4 * n:4 * n + w1_count(n), :],
                                      w1_bank(n)[:, 0:w1_count(n) * HID].rearrange("p (n h) -> p n h", h=HID)
                                      ).then_inc(w1_kept_dve, 1)

            def repeat_fields(t):
                dve.wait_ge(x_landed[t], 16 * FIELDS)
                if t:
                    dve.wait_ge(stack_turned, STACKS * CHUNKS * t)
                nc.vector.tensor_copy(x_rep.rearrange("p (r f) d -> p r (f d)", r=4),
                                      x_rows[:, t % 2:t % 2 + 1, :].to_broadcast([P, 4, FIELDS * DIM])
                                      ).then_inc(x_rep_done, 1)

            def form_pairs(s, n):
                fan, plain, blocks = TILES[n]
                rows = blocks * FIELDS
                at = s * PAIRS + n // 2
                dve.wait_ge(stack_kept, FANS * s + fan + 1)
                dve.wait_ge(stack_turned, STACKS * s + FANS + plain + 1)
                if at >= P_RING:
                    dve.wait_ge(hi_done, at - P_RING + 1)
                    dve.wait_ge(lo_done, at - P_RING + 1)
                nc.vector.tensor_tensor(
                    pairs[0:rows, at % P_RING, n % 2, :].rearrange("p (d b) -> p d b", b=P),
                    T[plain % 2][0:rows, :].rearrange("p (d b) -> p d b", b=P),
                    fan_chunk(fan, s, rows), ALU.mult).then_inc(pairs_done, 1)

            def rest_pairs(s, pair):
                tiles = min(2, NT - 2 * pair)
                rows = FIELDS * TILES[2 * pair][2]
                slot = pair_slot(s, pair)
                dve.wait_ge(hi_done, s * PAIRS + pair + 1)
                nc.vector.tensor_tensor(
                    pairs_lo[0:rows, slot, 0:tiles, :], pairs[0:rows, (s * PAIRS + pair) % P_RING, 0:tiles, :],
                    pairs_hi[0:rows, slot, 0:tiles, :].bitcast(F32), ALU.subtract).then_inc(lo_done, 1)

            def keep_h1(s):
                t, c = divmod(s, CHUNKS)
                dve.wait_ge(tile_used, NT * (s + 1))
                if t >= 2 and c == 0:
                    dve.wait_ge(rows_turned, 4 * (t - 1))
                dst = h1[:, t % 2, :].rearrange("p (b d) -> p d b", d=DIM)[:, c * CHUNK_D:(c + 1) * CHUNK_D, :]
                nc.vector.tensor_copy(dst, L[s % 2][:].rearrange("p (d b) -> p d b", b=P)).then_inc(h1_kept, 1)

            def side(u, k):
                if k in H_SLOT:
                    j = H_SLOT.index(k)
                    dve.wait_ge(rows_turned, 4 * u + j + 1)
                    if 4 * u + j >= 2:
                        dve.wait_ge(gram_done, 4 * (4 * u + j - 1))
                    nc.vector.tensor_copy(h1_rows[:, j % 2, :, :],
                                          H[:].rearrange("p (g q) -> p g q", q=HID)).then_inc(rows_kept, 1)
                if k == MLP1_SLOT:
                    dve.wait_ge(z2_done, u + 1)
                    if u:
                        dve.wait_ge(top1_done, u)
                    nc.vector.tensor_copy(z2_sb[:], M[:, 0:P]).then_inc(z2_kept, 1)
                if k == SLOTS:
                    dve.wait_ge(y_done, u + 1)
                    nc.vector.tensor_copy(y_sb[0:1, u * P:(u + 1) * P], M[0:1, 0:P]).then_inc(y_kept, 1)

            for s in range(-1, STEPS + CHUNKS):
                if s + 1 < STEPS and (s + 1) % CHUNKS == 0:
                    repeat_fields((s + 1) // CHUNKS)
                if 1 <= s <= STEPS:
                    keep_h1(s - 1)
                for n in range(NT):
                    if s + 1 < STEPS:
                        if n == 2:
                            form_pairs(s + 1, 0)
                            form_pairs(s + 1, 1)
                        if n == 3:
                            form_pairs(s + 1, 2)
                            form_pairs(s + 1, 3)
                            rest_pairs(s + 1, 0)
                        if n == 4:
                            form_pairs(s + 1, 4)
                            form_pairs(s + 1, 5)
                            rest_pairs(s + 1, 1)
                        if n == 5:
                            form_pairs(s + 1, 6)
                            rest_pairs(s + 1, 2)
                        if n == 6:
                            rest_pairs(s + 1, 3)
                    if s >= CHUNKS:
                        k = s % CHUNKS * NT + n
                        if k == 0 and s >= 2 * CHUNKS:
                            side(s // CHUNKS - 2, SLOTS)
                        side(s // CHUNKS - 1, k)
            side(BTILES - 1, SLOTS)

        @block.tensor
        def _(pe):
            pe.wait_ge(ident_done, 1)
            pe.wait_ge(w0_tiled, NT)
            for n, (fan, plain, blocks) in enumerate(TILES):
                last = nc.tensor.transpose(T[n // 4][0:blocks * FIELDS, (n % 4) * P:(n % 4 + 1) * P],
                                           w0_tiles[:, n, 0:blocks * FIELDS], ident[:])
                if n in (3, NT - 1):
                    last.then_inc(w0_turned, 1)
            pe.wait_ge(w1_in, 16)
            for n in range(WT_BANKS):
                if n >= 4:
                    pe.wait_ge(w1_kept_dve if n % 2 else w1_kept_act, kept_before(n - 4, n % 2))
                for j in range(w1_count(n)):
                    last = nc.tensor.transpose(w1_bank(n)[:, j * P:(j + 1) * P], w1_raw[:, 4 * n + j, :], ident[:])
                last.then_inc(w1_turned, 1)
            pe.wait_ge(small_in, 16 * SMALL_LOADS)
            for t in range(BTILES):
                last = nc.tensor.transpose(H[0:DENSE, t * P:(t + 1) * P], dense_sb[:, t, :], ident[:])
            last.then_inc(dense_turned, 1)

            def turn_stack(s, n):
                t, c = divmod(s, CHUNKS)
                if s == 0 and n == 0:
                    pe.wait_ge(w0_lo_done, len(W0_PARTS))
                if n < FANS and s:
                    pe.wait_ge(pairs_done, NT * (s - 1) + (6, NT)[n])
                elif FANS <= n < 2 * FANS:
                    pe.wait_ge(stack_kept, FANS * s + n - FANS + 1)
                elif n >= 2 * FANS:
                    pe.wait_ge(pairs_done, NT * s + FANS * (n - 2 * FANS + 1))
                if c == 0 and n < FANS:
                    pe.wait_ge(x_fan_done, FANS * t + n + 1)
                wide, first = (x_fan, n * ROWS) if n < FANS else (x_rep, PLAIN[n - FANS])
                for j in range(CHUNK_D):
                    last = nc.tensor.transpose(T[n % 2][0:ROWS, j * P:(j + 1) * P],
                                               wide[:, first:first + ROWS, c * CHUNK_D + j], ident[:])
                last.then_inc(stack_turned, 1)

            def layer1(s, n):
                rows = TILES[n][2] * FIELDS
                slot = pair_slot(s, n // 2)
                if n == 0 and s >= 2:
                    pe.wait_ge(h1_kept, s - 1)
                if n == 0 and s < 2:
                    pe.wait_ge(w1_kept_act, (WT_BANKS + 1) // 2)
                    pe.wait_ge(w1_kept_dve, WT_BANKS // 2)
                if n % 2 == 0:
                    pe.wait_ge(lo_done, s * PAIRS + n // 2 + 1)
                acc = L[s % 2][:]
                hi, lo = pairs_hi[0:rows, slot, n % 2, :], pairs_lo[0:rows, slot, n % 2, :]
                nc.tensor.matmul(acc, w0_hi[0:rows, n, :], hi, start=(n == 0), stop=False)
                nc.tensor.matmul(acc, w0_hi[0:rows, n, :], lo, start=False, stop=False)
                last = nc.tensor.matmul(acc, w0_lo[0:rows, n, :], hi, start=False, stop=(n == NT - 1))
                last.then_inc(tile_used, 1)

            def side(u, k):
                if k in XT_SLOT:
                    half = k - XT_SLOT[0]
                    if half:
                        pe.wait_ge(xcols_kept, 2 * u + 1)
                    elif u:
                        pe.wait_ge(y_kept, u)
                    for g in range(GROUPS // 2):
                        at = (half * GROUPS // 2 + g) * P
                        last = nc.tensor.transpose(M[:, g * FIELDS:(g + 1) * FIELDS],
                                                   fan0_tile(u)[0:FIELDS, at:at + P], ident[0:FIELDS, 0:FIELDS])
                    last.then_inc(xcols_turned, 1)
                if k in H_SLOT:
                    j = H_SLOT.index(k)
                    if j == 0:
                        pe.wait_ge(h1_kept, CHUNKS * (u + 1))
                    if u == 0 and j == 0:
                        pe.wait_ge(dense_kept, 1)
                    elif 4 * u + j:
                        pe.wait_ge(rows_kept, 4 * u + j)
                    for g in range(4):
                        at = (4 * j + g) * P
                        last = nc.tensor.transpose(H[:, g * P:(g + 1) * P], h1[:, u % 2, at:at + P], ident[:])
                    last.then_inc(rows_turned, 1)
                if G_SLOT <= k < G_SLOT + GROUPS:
                    g = k - G_SLOT
                    if g % 4 == 0:
                        pe.wait_ge(rows_kept, 4 * u + g // 4 + 1)
                    if g % (GROUPS // 2) == 0:
                        pe.wait_ge(xdiag_in[g // (GROUPS // 2)], 16 * GROUP * (u + 1))
                    if GROUPS * u + g >= 2:
                        pe.wait_ge(gram_kept, GROUPS * u + g - 1)
                    nc.tensor.matmul(G[g % 2][:, 0:GROUP * XF], h1_rows[:, g // 4 % 2, g % 4, :], x_diag[:, g, :],
                                     start=True, stop=True).then_inc(gram_done, 1)
                if Z2_SLOT <= k < Z2_SLOT + len(Z2_PARTS):
                    f0, f1 = Z2_PARTS[k - Z2_SLOT]
                    if f0 == 0:
                        pe.wait_ge(gram_kept, GROUPS * (u + 1))
                        pe.wait_ge(xcols_kept, 2 * u + 2)
                    for f in range(f0, f1):
                        last = nc.tensor.matmul(M[:, 0:P], w1_t[:, f, :], gram[:, f, :],
                                                start=(f == 0), stop=(f == FIELDS - 1))
                    if f1 == FIELDS:
                        last.then_inc(z2_done, 1)
                if k == MLP1_SLOT:
                    pe.wait_ge(z2_kept, u + 1)
                    for m in range(TOP1 // P):
                        cols = slice(m * P, (m + 1) * P)
                        nc.tensor.matmul(M[:, cols], wt1_z[:, 0, cols], gram[:, FIELDS, :], start=True, stop=False)
                        nc.tensor.matmul(M[:, cols], wt1_z[:, 1, cols], z2_sb[:], start=False, stop=False)
                        last = nc.tensor.matmul(M[:, cols], wt1_d[:, cols], dense_t[:, u * P:(u + 1) * P],
                                                start=False, stop=True)
                    last.then_inc(top1_done, 1)
                if k == MLP2_SLOT:
                    pe.wait_ge(top1_kept, TOP1 // P * (u + 1))
                    for m in range(TOP2 // P):
                        cols = slice(m * P, (m + 1) * P)
                        for j in range(TOP1 // P):
                            last = nc.tensor.matmul(M[:, cols], wt2_sb[:, j, cols], hid1[:, j, :],
                                                    start=(j == 0), stop=(j == TOP1 // P - 1))
                    last.then_inc(top2_done, 1)
                if k == SLOTS:
                    pe.wait_ge(top2_kept, TOP2 // P * (u + 1))
                    for j in range(TOP2 // P):
                        last = nc.tensor.matmul(M[0:1, 0:P], wt3_sb[:, j:j + 1], hid2[:, j, :],
                                                start=(j == 0), stop=(j == TOP2 // P - 1))
                    last.then_inc(y_done, 1)

            for s in range(-1, STEPS + CHUNKS):
                for n in range(NT):
                    if 0 <= s < STEPS:
                        layer1(s, n)
                    if s + 1 < STEPS and n < STACKS:
                        turn_stack(s + 1, n)
                    if s >= CHUNKS:
                        k = s % CHUNKS * NT + n
                        if k == 0 and s >= 2 * CHUNKS:
                            side(s // CHUNKS - 2, SLOTS)
                        side(s // CHUNKS - 1, k)
            side(BTILES - 1, SLOTS)


def kernel(**inputs):
    import concourse.bacc as _bacc
    from concourse.bass_utils import run_bass_kernel_spmd as _run

    nc = _bacc.Bacc("TRN2", target_bir_lowering=False, num_devices=1)
    arrays = {}

    def dram(name, a, dt=F32):
        arrays[name] = np.ascontiguousarray(a)
        return nc.dram_tensor(name, arrays[name].shape, dt, kind="ExternalInput").ap()

    ids = dram("ids", np.asarray(inputs["ids"]).reshape(BTILES, P, FIELDS).transpose(1, 0, 2), I32)
    tables = [dram(f"tbl_{f}", inputs[f"tbl_{f}"]) for f in range(FIELDS)]
    dense = dram("dense", inputs["dense_ctx"])
    w0 = dram("w0", np.asarray(inputs["L0_rec_W0"]).reshape(HID, FIELDS, FIELDS))
    w1 = dram("w1", np.asarray(inputs["L0_rec_W1"]).reshape(HID, FIELDS, HID))
    wt1 = dram("wt1", inputs["W_top1"])
    b1 = dram("b1", np.asarray(inputs["b_top1"]).reshape(TOP1 // P, P).T)
    wt2 = dram("wt2", inputs["W_top2"])
    b2 = dram("b2", np.asarray(inputs["b_top2"]).reshape(TOP2 // P, P).T)
    wt3 = dram("wt3", np.asarray(inputs["W_top3"]).reshape(TOP2 // P, P).T)
    out = nc.dram_tensor("y", (1, BATCH), F32, kind="ExternalOutput").ap()
    build(nc, ids, tables, dense, w0, w1, wt1, b1, wt2, b2, wt3, out)
    r = _run(nc, [arrays], core_ids=[0])
    return np.asarray(r.results[0]["y"]).reshape(BATCH, 1)
```

```python
from contextlib import ExitStack

import numpy as np

import concourse.bass as bass
from concourse import mybir

F32 = mybir.dt.float32
F32R = mybir.dt.float32r
I32 = mybir.dt.int32
U32 = mybir.dt.uint32
ALU = mybir.AluOpType
ACT = mybir.ActivationFunctionType

P = 128
BATCH = 512
FIELDS = 39
DIM = 16
HID = 128
DENSE = 16
TOP1 = 512
TOP2 = 256
BTILES = BATCH // P

BLOCKS = 3
ROWS = BLOCKS * FIELDS
PLAIN = (0, 3, 6, 9)
FANS = (9, 21)
TILES = ((0, 0, 3), (0, 1, 3), (0, 2, 3), (0, 3, 3), (1, 3, 3), (1, 2, 3), (1, 1, 2))
NT = len(TILES)


def covered_differences():
    out = []
    for fan, plain, blocks in TILES:
        for j in range(blocks):
            gap = (FANS[fan] + j - PLAIN[plain]) % FIELDS
            out.append(min(gap, FIELDS - gap))
    return sorted(out)


assert covered_differences() == list(range(FIELDS // 2 + 1))

CHUNK_D = 4
CHUNKS = DIM // CHUNK_D
COLS = CHUNK_D * P
STEPS = BTILES * CHUNKS
SLOTS = CHUNKS * NT
GROUP = P // DIM
GROUPS = P // GROUP
HALVES = 2
SHARE = GROUP // HALVES
HROWS = P // HALVES
BATCH_G = 4
BATCHES = GROUPS // BATCH_G
BANK_G = 2
SUBS = BATCH_G // BANK_G
XF = FIELDS + 1

SPLIT = 4
SPAIRS = SPLIT // 2
DIRECT = NT - SPLIT
P_RING = 2
SPLIT_RING = 5
DIRECT_RING = 5

TURN_AT = 1
ROUND_AT = (1, 3)
XT_SLOT = (23, 25)
Z2_SLOT = 2
Z2_PARTS = tuple((f, min(f + 3, FIELDS)) for f in range(0, FIELDS, 3))
Z2_END = Z2_SLOT + len(Z2_PARTS) - 1
MLP1_SLOT = Z2_END + 2
MLP2_SLOT = MLP1_SLOT + 2
MLP3_SLOT = MLP2_SLOT + 2
assert MLP3_SLOT < XT_SLOT[0]
WT_BANKS = (FIELDS + 3) // 4


def build(nc, ids, tables, dense, w0, w1, wt1, b1, wt2, b2, wt3, out):
    with ExitStack() as ctx:
        def sb(name, shape, dt=F32):
            return ctx.enter_context(nc.sbuf_tensor(name, shape, dt))

        def bank(name):
            return ctx.enter_context(nc.psum_tensor(name, [P, 512], F32))

        def sem(name):
            return ctx.enter_context(nc.semaphore(name))

        MADE = len(PLAIN) - 1 + len(FANS)

        idx = sb("idx", [P, BTILES, FIELDS], I32)
        x_rows = sb("x_rows", [P, 2, FIELDS * DIM])
        x_rep = sb("x_rep", [P, P, DIM])
        ident = sb("ident", [P, P])
        x_turned = sb("x_turned", [P, 2, COLS])
        stacks = sb("stacks", [P, 2 * MADE * COLS + P * DIM])
        pairs = sb("pairs", [P, P_RING, 2, COLS])
        direct = sb("direct", [P, DIRECT_RING, COLS])
        pairs_hi = sb("pairs_hi", [P, SPLIT_RING, 2, COLS], F32R)
        pairs_lo = sb("pairs_lo", [P, SPLIT_RING, 2, COLS], F32R)
        w0_hi = sb("w0_hi", [P, SPLIT, P], F32R)
        w0_lo = sb("w0_lo", [P, SPLIT, P], F32R)
        w0_direct = sb("w0_direct", [P, DIRECT, P])
        w1_t = sb("w1_t", [P, FIELDS, P])
        h1 = sb("h1", [P, P * DIM])
        h1_rows = sb("h1_rows", [P, 2, 4, P])
        own = sb("own", [P, SHARE])
        x_diag = sb("x_diag", [P, GROUPS, SHARE, XF])
        gram = sb("gram", [P, XF, P])
        z2_sb = sb("z2_sb", [P, P])
        dense_sb = sb("dense_sb", [P, BTILES, DENSE])
        dense_t = sb("dense_t", [DENSE, BATCH])
        wt1_z = sb("wt1_z", [P, 2, TOP1])
        wt1_d = sb("wt1_d", [DENSE, TOP1])
        wt2_sb = sb("wt2_sb", [P, TOP1 // P, TOP2])
        wt3_sb = sb("wt3_sb", [P, TOP2 // P])
        b1_sb = sb("b1_sb", [P, TOP1 // P])
        b2_sb = sb("b2_sb", [P, TOP2 // P])
        hid1 = sb("hid1", [P, TOP1 // P, P])
        hid2 = sb("hid2", [P, TOP2 // P, P])
        y_sb = sb("y_sb", [1, BATCH])

        x_tile = stacks[0:FIELDS, 2 * MADE * COLS:]

        def made(i, s, rows):
            at = (s % 2 * MADE + i) * COLS
            return stacks[rows, at:at + COLS]

        def plain_stack(plain, s, rows):
            return made(plain - 1, s, rows) if plain else x_turned[rows, s % 2, :]

        def fan_stack(fan, s, rows):
            return made(len(PLAIN) - 1 + fan, s, rows)

        direct_space = direct[:].rearrange("p r n -> p (r n)")
        wsym = stacks[:, 0:4 * FIELDS * FIELDS].rearrange("p (f q) -> p f q", q=2 * FIELDS)
        w0_raw = h1[:, 0:FIELDS * FIELDS].rearrange("p (f q) -> p f q", q=FIELDS)
        w0_tiles = direct_space[:, 0:NT * ROWS].rearrange("p (n r) -> p n r", r=ROWS)
        w1_raw = gram[:].rearrange("p f q -> p (f q)")[:, 0:FIELDS * HID].rearrange(
            "p (f q) -> p f q", q=HID)

        T = bank("turn_bank")
        L = [bank("layer1_bank0"), bank("layer1_bank1")]
        M = bank("tower_bank")
        G = [bank(f"gram_bank{i}") for i in range(SUBS * HALVES)]

        ids_in = sem("ids_in")
        w0_in = sem("w0_in")
        w1_in = sem("w1_in")
        small_in = sem("small_in")
        x_landed = [sem(f"x_landed{t}") for t in range(BTILES)]
        ident_zero = sem("ident_zero")
        ident_done = sem("ident_done")
        sym_done = sem("sym_done")
        w0_tiled = sem("w0_tiled")
        own_done = sem("own_done")
        ones_done = sem("ones_done")
        w0_turned = sem("w0_turned")
        w0_hi_done = sem("w0_hi_done")
        w0_direct_done = sem("w0_direct_done")
        w0_lo_done = sem("w0_lo_done")
        w1_turned = sem("w1_turned")
        w1_kept_act = sem("w1_kept_act")
        w1_kept_dve = sem("w1_kept_dve")
        dense_turned = sem("dense_turned")
        dense_kept = sem("dense_kept")
        x_rep_done = sem("x_rep_done")
        x_turned_done = sem("x_turned_done")
        x_turned_kept = sem("x_turned_kept")
        x_tile_kept = sem("x_tile_kept")
        stack_in = [[sem(f"stack{i}_in{slot}") for i in range(MADE)] for slot in range(2)]
        split_formed = sem("split_formed")
        direct_formed = sem("direct_formed")
        hi_done = sem("hi_done")
        lo_done = sem("lo_done")
        tile_used = sem("tile_used")
        h1_kept = sem("h1_kept")
        xcols_turned = sem("xcols_turned")
        xdiag_kept = sem("xdiag_kept")
        rows_turned = sem("rows_turned")
        rows_kept = sem("rows_kept")
        gram_done = sem("gram_done")
        gram_kept = sem("gram_kept")
        z2_done = sem("z2_done")
        z2_kept = sem("z2_kept")
        top1_done = sem("top1_done")
        top1_kept = sem("top1_kept")
        top2_done = sem("top2_done")
        top2_kept = sem("top2_kept")
        y_done = sem("y_done")
        y_kept = sem("y_kept")
        y_out = sem("y_out")

        SMALL_LOADS = 7

        def tile_rows(n):
            return TILES[n][2] * FIELDS

        W0_PARTS = ((0, SPLIT, L[0]), (SPLIT, NT - 1, L[1]), (NT - 1, NT, L[1]))

        def w0_bank(n0, n1, bank_):
            first = 0 if n0 < SPLIT else SPLIT
            cols = bank_[0:tile_rows(n0), (n0 - first) * HID:(n1 - first) * HID]
            return cols.rearrange("p (n h) -> p n h", h=HID)

        def w1_bank(n):
            return G[n % 4]

        def w1_count(n):
            return min(4, FIELDS - 4 * n)

        def kept_before(n, parity):
            return (n - parity) // 2 + 1

        def pair_slot(s, pair):
            return (s * SPAIRS + pair) % SPLIT_RING

        def direct_slot(s, n):
            return (s * DIRECT + n - SPLIT) % DIRECT_RING

        def used_when_free(at, per_chunk, ring, last_tile):
            s, i = divmod(at - ring, per_chunk)
            return NT * s + last_tile(i) + 1

        block = ctx.enter_context(nc.Block())

        @block.sync
        def _(sp):
            sp.dma_start(idx[:], ids).then_inc(ids_in, 16)
            sp.dma_start(w0_raw, w0).then_inc(w0_in, 16)
            sp.dma_start(w1_raw, w1).then_inc(w1_in, 16)
            sp.dma_start(dense_sb[:], dense.rearrange("(t p) c -> p t c", p=P)).then_inc(small_in, 16)
            sp.dma_start(wt1_z[:], wt1[0:2 * HID, :].rearrange("(k p) n -> p k n", p=P)).then_inc(small_in, 16)
            sp.dma_start(wt1_d[:], wt1[2 * HID:2 * HID + DENSE, :]).then_inc(small_in, 16)
            sp.dma_start(wt2_sb[:], wt2.rearrange("(k p) n -> p k n", p=P)).then_inc(small_in, 16)
            sp.dma_start(wt3_sb[:], wt3).then_inc(small_in, 16)
            sp.dma_start(b1_sb[:], b1).then_inc(small_in, 16)
            sp.dma_start(b2_sb[:], b2).then_inc(small_in, 16)

            def make_stacks(s):
                sp.wait_ge(x_turned_kept, s + 1)
                if s >= 2:
                    sp.wait_ge(split_formed, SPLIT * (s - 1))
                    sp.wait_ge(direct_formed, DIRECT * (s - 1))

                def make_fan(fan):
                    for j in range(BLOCKS):
                        first = FANS[fan] + j
                        sp.dma_start(fan_stack(fan, s, slice(j * FIELDS, (j + 1) * FIELDS)),
                                     x_turned[first:first + FIELDS, s % 2, :]
                                     ).then_inc(stack_in[s % 2][len(PLAIN) - 1 + fan], 16)

                make_fan(0)
                for plain in range(1, len(PLAIN)):
                    sp.dma_start(plain_stack(plain, s, slice(0, ROWS)),
                                 x_turned[PLAIN[plain]:PLAIN[plain] + ROWS, s % 2, :]
                                 ).then_inc(stack_in[s % 2][plain - 1], 16)
                make_fan(1)

            for s in range(STEPS):
                make_stacks(s)
            sp.wait_ge(y_kept, BTILES)
            sp.dma_start(out, y_sb[:]).then_inc(y_out, 16)
            sp.wait_ge(y_out, 16)

        @block.gpsimd
        def _(pool):
            nc.gpsimd.memset(ident[:], 0.0).then_inc(ident_zero, 1)
            pool.wait_ge(ident_zero, 1)
            nc.gpsimd.affine_select(out=ident[:], in_=ident[:], compare_op=ALU.not_equal, fill=1.0,
                                    base=0, pattern=[[-1, P]], channel_multiplier=1).then_inc(ident_done, 1)
            pool.wait_ge(ids_in, 16)
            for t in range(BTILES):
                if t >= 2:
                    pool.wait_ge(x_rep_done, 2 * (t - 1))
                for f in range(FIELDS):
                    nc.gpsimd.indirect_dma_start(
                        out=x_rows[:, t % 2, f * DIM:(f + 1) * DIM], out_offset=None, in_=tables[f],
                        in_offset=bass.IndirectOffsetOnAxis(ap=idx[:, t, f:f + 1].bitcast(U32), axis=0),
                    ).then_inc(x_landed[t], 16)

        @block.scalar
        def _(act):
            act.wait_ge(w0_turned, 1)
            n0, n1, bank_ = W0_PARTS[0]
            nc.scalar.activation(w0_hi[0:ROWS, :, :], w0_bank(n0, n1, bank_), ACT.Copy).then_inc(w0_hi_done, 1)
            act.wait_ge(w0_turned, 2)
            for n0, n1, bank_ in W0_PARTS[1:]:
                nc.scalar.activation(w0_direct[0:tile_rows(n0), n0 - SPLIT:n1 - SPLIT, :], w0_bank(n0, n1, bank_),
                                     ACT.Copy).then_inc(w0_direct_done, 1)
            for n in range(0, WT_BANKS, 2):
                act.wait_ge(w1_turned, n + 1)
                nc.scalar.activation(w1_t[:, 4 * n:4 * n + w1_count(n), :],
                                     w1_bank(n)[:, 0:w1_count(n) * HID].rearrange("p (n h) -> p n h", h=HID),
                                     ACT.Copy).then_inc(w1_kept_act, 1)
            act.wait_ge(dense_turned, 1)
            nc.scalar.activation(dense_t[:], M[0:DENSE, :], ACT.Copy).then_inc(dense_kept, 1)

            def keep_turned(s):
                t, c = divmod(s, CHUNKS)
                act.wait_ge(x_turned_done, s + 1)
                if s >= 2:
                    act.wait_ge(split_formed, SPLIT * (s - 1))
                    act.wait_ge(direct_formed, DIRECT * (s - 1))
                nc.scalar.activation(x_turned[:, s % 2, :], T[:], ACT.Copy).then_inc(x_turned_kept, 1)
                if t and c == 0:
                    act.wait_ge(xcols_turned, 2 * t)
                dst = x_tile.rearrange("p (b d) -> p d b", d=DIM)[:, c * CHUNK_D:(c + 1) * CHUNK_D, :]
                nc.scalar.activation(dst, T[0:FIELDS, :].rearrange("p (d b) -> p d b", b=P),
                                     ACT.Copy).then_inc(x_tile_kept, 1)

            def keep_h1(s):
                t, c = divmod(s, CHUNKS)
                act.wait_ge(tile_used, NT * (s + 1))
                if t and c == 0:
                    act.wait_ge(rows_turned, BATCHES * t)
                dst = h1[:].rearrange("p (b d) -> p d b", d=DIM)[:, c * CHUNK_D:(c + 1) * CHUNK_D, :]
                nc.scalar.activation(dst, L[s % 2][:].rearrange("p (d b) -> p d b", b=P),
                                     ACT.Copy).then_inc(h1_kept, 1)

            def round_pairs(s, pair):
                at = s * SPAIRS + pair
                act.wait_ge(split_formed, 2 * (at + 1))
                if at >= SPLIT_RING:
                    act.wait_ge(tile_used, used_when_free(at, SPAIRS, SPLIT_RING, lambda i: 2 * i + 1))
                nc.scalar.activation(pairs_hi[0:ROWS, pair_slot(s, pair), :, :], pairs[0:ROWS, at % P_RING, :, :],
                                     ACT.Copy).then_inc(hi_done, 1)

            def keep_xdiag(u, half):
                g0 = half * GROUPS // 2
                act.wait_ge(xcols_turned, 2 * u + half + 1)
                if u == 0:
                    act.wait_ge(own_done, 1)
                else:
                    act.wait_ge(gram_done, SUBS * BATCHES * u)
                for b in range(SHARE):
                    nc.scalar.activation(
                        x_diag[:, g0:g0 + GROUPS // 2, b, 0:FIELDS],
                        M[:, 0:GROUPS // 2 * FIELDS].rearrange("p (g f) -> p g f", f=FIELDS),
                        ACT.Copy, scale=own[:, b:b + 1]).then_inc(xdiag_kept, 1)

            def keep_rows(u, j):
                act.wait_ge(rows_turned, BATCHES * u + j + 1)
                if BATCHES * u + j >= 2:
                    act.wait_ge(gram_done, SUBS * (BATCHES * u + j - 1))
                nc.scalar.activation(h1_rows[:, j % 2, :, :], M[:].rearrange("p (g q) -> p g q", q=HID),
                                     ACT.Copy).then_inc(rows_kept, 1)

            def keep_gram(u, j):
                if u and j == 0:
                    act.wait_ge(top1_done, u)
                to = gram[:].rearrange("p f (g i b) -> p g i b f", i=HALVES, b=SHARE)
                for sub in range(SUBS):
                    g0 = j * BATCH_G + sub * BANK_G
                    act.wait_ge(gram_done, SUBS * (BATCHES * u + j) + sub + 1)
                    for i in range(HALVES):
                        nc.scalar.activation(
                            to[:, g0:g0 + BANK_G, i, :, :],
                            G[sub * HALVES + i][:, 0:BANK_G * SHARE * XF].rearrange(
                                "p (g b f) -> p g b f", b=SHARE, f=XF),
                            ACT.Copy).then_inc(gram_kept, 1)

            def tower(u, k):
                if k == Z2_END:
                    act.wait_ge(z2_done, u + 1)
                    if u:
                        act.wait_ge(top1_done, u)
                    nc.scalar.activation(z2_sb[:], M[:, 0:P], ACT.Copy).then_inc(z2_kept, 1)
                if k == MLP1_SLOT:
                    act.wait_ge(top1_done, u + 1)
                    if u == 0:
                        act.wait_ge(small_in, 16 * SMALL_LOADS)
                    else:
                        act.wait_ge(top2_done, u)
                    for m in range(TOP1 // P):
                        nc.scalar.activation(hid1[:, m, :], M[:, m * P:(m + 1) * P], ACT.Relu,
                                             bias=b1_sb[:, m:m + 1]).then_inc(top1_kept, 1)
                if k == MLP2_SLOT:
                    act.wait_ge(top2_done, u + 1)
                    if u:
                        act.wait_ge(y_done, u)
                    for m in range(TOP2 // P):
                        nc.scalar.activation(hid2[:, m, :], M[:, m * P:(m + 1) * P], ACT.Relu,
                                             bias=b2_sb[:, m:m + 1]).then_inc(top2_kept, 1)
                if k == MLP3_SLOT:
                    act.wait_ge(y_done, u + 1)
                    nc.scalar.activation(y_sb[0:1, u * P:(u + 1) * P], M[0:1, 0:P], ACT.Copy).then_inc(y_kept, 1)

            def gram_stage(u, t):
                keep_h1(CHUNKS * (u + 1) - 1)
                if t < BTILES:
                    keep_turned(CHUNKS * t)
                keep_rows(u, 0)
                keep_rows(u, 1)
                if t < BTILES:
                    keep_turned(CHUNKS * t + 1)
                for j in range(BATCHES):
                    keep_gram(u, j)
                    if j + 2 < BATCHES:
                        keep_rows(u, j + 2)
                    if t < BTILES and 1 <= j <= SPAIRS:
                        round_pairs(CHUNKS * t, j - 1)

            keep_turned(0)
            keep_turned(1)
            for t in range(BTILES):
                if t:
                    gram_stage(t - 1, t)
                else:
                    for pair in range(SPAIRS):
                        round_pairs(0, pair)
                for c in range(CHUNKS):
                    s = CHUNKS * t + c
                    for n in range(NT):
                        if n == 0 and c:
                            keep_h1(s - 1)
                        if n in ROUND_AT and c + 1 < CHUNKS:
                            round_pairs(s + 1, ROUND_AT.index(n))
                        if n == TURN_AT and c + 2 < CHUNKS:
                            keep_turned(s + 2)
                        if t:
                            tower(t - 1, c * NT + n)
                        if c * NT + n in XT_SLOT:
                            keep_xdiag(t, XT_SLOT.index(c * NT + n))
            gram_stage(BTILES - 1, BTILES)
            for k in (Z2_END, MLP1_SLOT, MLP2_SLOT, MLP3_SLOT):
                tower(BTILES - 1, k)

        @block.vector
        def _(dve):
            dve.wait_ge(ident_done, 1)
            nc.vector.tensor_reduce(own[:], ident[:].rearrange("p (i b d) -> p b i d", b=SHARE, d=DIM),
                                    mybir.AxisListType.XY, ALU.add).then_inc(own_done, 1)
            dve.wait_ge(own_done, 1)
            for b in range(SHARE):
                nc.vector.tensor_copy(x_diag[:, :, b, FIELDS], own[:, b:b + 1].to_broadcast([P, GROUPS])
                                      ).then_inc(ones_done, 1)
            dve.wait_ge(w0_in, 16)
            corner = wsym[:, 0:FIELDS, 0:FIELDS]
            nc.vector.tensor_tensor(corner, w0_raw, w0_raw.rearrange("p f q -> p q f"), ALU.add).then_inc(sym_done, 1)
            dve.wait_ge(sym_done, 1)
            diagonal = bass.AP(tensor=corner.tensor, offset=corner.offset,
                               ap=[list(corner.ap[0]), [2 * FIELDS + 1, FIELDS]])
            nc.vector.tensor_scalar(diagonal, diagonal, 0.5, None, ALU.mult).then_inc(sym_done, 1)
            dve.wait_ge(sym_done, 2)
            nc.vector.tensor_copy(wsym[:, 0:FIELDS, FIELDS:2 * FIELDS], corner).then_inc(sym_done, 1)
            dve.wait_ge(sym_done, 3)
            nc.vector.tensor_copy(wsym[:, FIELDS:2 * FIELDS, :], wsym[:, 0:FIELDS, :]).then_inc(sym_done, 1)
            for n, (fan, plain, blocks) in enumerate(TILES):
                dve.wait_ge(sym_done, 4)
                at = wsym[:, FANS[fan], PLAIN[plain]:PLAIN[plain] + 1]
                rows = bass.AP(tensor=at.tensor, offset=at.offset,
                               ap=[list(at.ap[0]), [2 * FIELDS, blocks], [2 * FIELDS + 1, FIELDS]])
                nc.vector.tensor_copy(w0_tiles[:, n, 0:blocks * FIELDS].rearrange("p (j f) -> p j f", j=blocks),
                                      rows).then_inc(w0_tiled, 1)
            dve.wait_ge(w0_hi_done, 1)
            nc.vector.tensor_tensor(w0_lo[0:ROWS, :, :], w0_bank(*W0_PARTS[0]),
                                    w0_hi[0:ROWS, :, :].bitcast(F32), ALU.subtract).then_inc(w0_lo_done, 1)
            for n in range(1, WT_BANKS, 2):
                dve.wait_ge(w1_turned, n + 1)
                nc.vector.tensor_copy(w1_t[:, 4 * n:4 * n + w1_count(n), :],
                                      w1_bank(n)[:, 0:w1_count(n) * HID].rearrange("p (n h) -> p n h", h=HID)
                                      ).then_inc(w1_kept_dve, 1)

            def repeat_fields(t):
                dve.wait_ge(x_landed[t], 16 * FIELDS)
                if t:
                    dve.wait_ge(x_turned_done, CHUNKS * t)
                whole = P // FIELDS
                nc.vector.tensor_copy(x_rep[:, 0:whole * FIELDS, :].rearrange("p (r f) d -> p r (f d)", r=whole),
                                      x_rows[:, t % 2:t % 2 + 1, :].to_broadcast([P, whole, FIELDS * DIM])
                                      ).then_inc(x_rep_done, 1)
                nc.vector.tensor_copy(x_rep[:, whole * FIELDS:, :].rearrange("p f d -> p (f d)"),
                                      x_rows[:, t % 2, 0:(P - whole * FIELDS) * DIM]).then_inc(x_rep_done, 1)

            def form_pairs(s, n):
                fan, plain, blocks = TILES[n]
                rows = blocks * FIELDS
                uses = s // 2 + 1
                dve.wait_ge(stack_in[s % 2][len(PLAIN) - 1 + fan], 16 * BLOCKS * uses)
                if plain:
                    dve.wait_ge(stack_in[s % 2][plain - 1], 16 * uses)
                if n < SPLIT:
                    at = s * SPAIRS + n // 2
                    if at >= P_RING:
                        dve.wait_ge(hi_done, at - P_RING + 1)
                        dve.wait_ge(lo_done, at - P_RING + 1)
                    to = pairs[0:rows, at % P_RING, n % 2, :]
                else:
                    at = s * DIRECT + n - SPLIT
                    if at >= DIRECT_RING:
                        dve.wait_ge(tile_used, used_when_free(at, DIRECT, DIRECT_RING, lambda i: SPLIT + i))
                    to = direct[0:rows, direct_slot(s, n), :]
                nc.vector.tensor_tensor(to, plain_stack(plain, s, slice(0, rows)), fan_stack(fan, s, slice(0, rows)),
                                        ALU.mult).then_inc(split_formed if n < SPLIT else direct_formed, 1)

            def rest_pairs(s, pair):
                at = s * SPAIRS + pair
                slot = pair_slot(s, pair)
                dve.wait_ge(hi_done, at + 1)
                nc.vector.tensor_tensor(pairs_lo[0:ROWS, slot, :, :], pairs[0:ROWS, at % P_RING, :, :],
                                        pairs_hi[0:ROWS, slot, :, :].bitcast(F32), ALU.subtract).then_inc(lo_done, 1)

            for s in range(STEPS):
                if s % CHUNKS == 0:
                    repeat_fields(s // CHUNKS)
                for n in range(NT):
                    form_pairs(s, n)
                    if n % 2 and 2 < n:
                        if n // 2 - 1 < SPAIRS:
                            rest_pairs(s, n // 2 - 1)

        @block.tensor
        def _(pe):
            pe.wait_ge(ident_done, 1)
            pe.wait_ge(w0_tiled, NT)
            for n, (fan, plain, blocks) in enumerate(TILES):
                to, at = (L[0], n) if n < SPLIT else (L[1], n - SPLIT)
                last = nc.tensor.transpose(to[0:blocks * FIELDS, at * P:(at + 1) * P],
                                           w0_tiles[:, n, 0:blocks * FIELDS], ident[:])
                if n in (SPLIT - 1, NT - 1):
                    last.then_inc(w0_turned, 1)
            pe.wait_ge(w1_in, 16)
            for n in range(WT_BANKS):
                if n >= 4:
                    pe.wait_ge(w1_kept_dve if n % 2 else w1_kept_act, kept_before(n - 4, n % 2))
                for j in range(w1_count(n)):
                    last = nc.tensor.transpose(w1_bank(n)[:, j * P:(j + 1) * P], w1_raw[:, 4 * n + j, :], ident[:])
                last.then_inc(w1_turned, 1)
            pe.wait_ge(small_in, 16 * SMALL_LOADS)
            for t in range(BTILES):
                last = nc.tensor.transpose(M[0:DENSE, t * P:(t + 1) * P], dense_sb[:, t, :], ident[:])
            last.then_inc(dense_turned, 1)

            def turn_x(s):
                t, c = divmod(s, CHUNKS)
                if s:
                    pe.wait_ge(x_tile_kept, s)
                if c == 0:
                    pe.wait_ge(x_rep_done, 2 * (t + 1))
                for j in range(CHUNK_D):
                    last = nc.tensor.transpose(T[:, j * P:(j + 1) * P], x_rep[:, :, c * CHUNK_D + j], ident[:])
                last.then_inc(x_turned_done, 1)

            def layer1(s, n):
                rows = TILES[n][2] * FIELDS
                if s == 0 and n == 0:
                    pe.wait_ge(w0_lo_done, 1)
                    pe.wait_ge(w0_direct_done, len(W0_PARTS) - 1)
                if n == 0 and s >= 2:
                    pe.wait_ge(h1_kept, s - 1)
                acc = L[s % 2][:]
                if n < SPLIT:
                    slot = pair_slot(s, n // 2)
                    if n % 2 == 0:
                        pe.wait_ge(lo_done, s * SPAIRS + n // 2 + 1)
                    hi, lo = pairs_hi[0:rows, slot, n % 2, :], pairs_lo[0:rows, slot, n % 2, :]
                    nc.tensor.matmul(acc, w0_hi[0:rows, n, :], hi, start=(n == 0), stop=False)
                    nc.tensor.matmul(acc, w0_hi[0:rows, n, :], lo, start=False, stop=False)
                    last = nc.tensor.matmul(acc, w0_lo[0:rows, n, :], hi, start=False, stop=(n == NT - 1))
                else:
                    pe.wait_ge(direct_formed, s * DIRECT + n - SPLIT + 1)
                    last = nc.tensor.matmul(acc, w0_direct[0:rows, n - SPLIT, :], direct[0:rows, direct_slot(s, n), :],
                                            start=False, stop=(n == NT - 1))
                last.then_inc(tile_used, 1)

            def turn_xcols(u, half):
                pe.wait_ge(x_tile_kept, CHUNKS * (u + 1))
                if half:
                    pe.wait_ge(xdiag_kept, SHARE * (2 * u + 1))
                elif u:
                    pe.wait_ge(y_kept, u)
                else:
                    pe.wait_ge(dense_kept, 1)
                for g in range(GROUPS // 2):
                    at = (half * GROUPS // 2 + g) * P
                    last = nc.tensor.transpose(M[:, g * FIELDS:(g + 1) * FIELDS], x_tile[:, at:at + P],
                                               ident[0:FIELDS, 0:FIELDS])
                last.then_inc(xcols_turned, 1)

            def turn_h1(u, j):
                if j == 0:
                    pe.wait_ge(h1_kept, CHUNKS * (u + 1))
                if j:
                    pe.wait_ge(rows_kept, BATCHES * u + j)
                else:
                    pe.wait_ge(xdiag_kept, SHARE * 2 * (u + 1))
                for g in range(BATCH_G):
                    at = (BATCH_G * j + g) * P
                    last = nc.tensor.transpose(M[:, g * P:(g + 1) * P], h1[:, at:at + P], ident[:])
                last.then_inc(rows_turned, 1)

            def form_gram(u, j):
                if u == 0 and j == 0:
                    pe.wait_ge(ones_done, SHARE)
                    pe.wait_ge(w1_kept_act, (WT_BANKS + 1) // 2)
                    pe.wait_ge(w1_kept_dve, WT_BANKS // 2)
                pe.wait_ge(rows_kept, BATCHES * u + j + 1)
                for sub in range(SUBS):
                    at = SUBS * (BATCHES * u + j) + sub
                    if at >= SUBS:
                        pe.wait_ge(gram_kept, HALVES * (at - SUBS + 1))
                    for b in range(BANK_G):
                        g = sub * BANK_G + b
                        for i in range(HALVES):
                            rows = slice(i * HROWS, (i + 1) * HROWS)
                            last = nc.tensor.matmul(
                                G[sub * HALVES + i][:, b * SHARE * XF:(b + 1) * SHARE * XF],
                                h1_rows[rows, j % 2, g, :], x_diag[rows, BATCH_G * j + g, :, :],
                                start=True, stop=True)
                    last.then_inc(gram_done, 1)

            def gram_stage(u, t):
                if t < BTILES:
                    turn_x(CHUNKS * t)
                turn_h1(u, 0)
                turn_h1(u, 1)
                if t < BTILES:
                    turn_x(CHUNKS * t + 1)
                for j in range(BATCHES):
                    form_gram(u, j)
                    if j + 2 < BATCHES:
                        turn_h1(u, j + 2)

            def tower(u, k):
                if Z2_SLOT <= k <= Z2_END:
                    f0, f1 = Z2_PARTS[k - Z2_SLOT]
                    if f0 == 0:
                        pe.wait_ge(gram_kept, HALVES * SUBS * BATCHES * (u + 1))
                    for f in range(f0, f1):
                        last = nc.tensor.matmul(M[:, 0:P], w1_t[:, f, :], gram[:, f, :],
                                                start=(f == 0), stop=(f == FIELDS - 1))
                    if f1 == FIELDS:
                        last.then_inc(z2_done, 1)
                if k == MLP1_SLOT:
                    pe.wait_ge(z2_kept, u + 1)
                    for m in range(TOP1 // P):
                        cols = slice(m * P, (m + 1) * P)
                        nc.tensor.matmul(M[:, cols], wt1_z[:, 0, cols], gram[:, FIELDS, :], start=True, stop=False)
                        nc.tensor.matmul(M[:, cols], wt1_z[:, 1, cols], z2_sb[:], start=False, stop=False)
                        last = nc.tensor.matmul(M[:, cols], wt1_d[:, cols], dense_t[:, u * P:(u + 1) * P],
                                                start=False, stop=True)
                    last.then_inc(top1_done, 1)
                if k == MLP2_SLOT:
                    pe.wait_ge(top1_kept, TOP1 // P * (u + 1))
                    for m in range(TOP2 // P):
                        cols = slice(m * P, (m + 1) * P)
                        for j in range(TOP1 // P):
                            last = nc.tensor.matmul(M[:, cols], wt2_sb[:, j, cols], hid1[:, j, :],
                                                    start=(j == 0), stop=(j == TOP1 // P - 1))
                    last.then_inc(top2_done, 1)
                if k == MLP3_SLOT:
                    pe.wait_ge(top2_kept, TOP2 // P * (u + 1))
                    for j in range(TOP2 // P):
                        last = nc.tensor.matmul(M[0:1, 0:P], wt3_sb[:, j:j + 1], hid2[:, j, :],
                                                start=(j == 0), stop=(j == TOP2 // P - 1))
                    last.then_inc(y_done, 1)

            turn_x(0)
            turn_x(1)
            for t in range(BTILES):
                if t:
                    gram_stage(t - 1, t)
                for c in range(CHUNKS):
                    s = CHUNKS * t + c
                    for n in range(NT):
                        layer1(s, n)
                        if n == TURN_AT and c + 2 < CHUNKS:
                            turn_x(s + 2)
                        if t:
                            tower(t - 1, c * NT + n)
                        if c * NT + n in XT_SLOT:
                            turn_xcols(t, XT_SLOT.index(c * NT + n))
            gram_stage(BTILES - 1, BTILES)
            for k in range(Z2_SLOT, MLP3_SLOT + 1):
                tower(BTILES - 1, k)


def kernel(**inputs):
    import concourse.bacc as _bacc
    from concourse.bass_utils import run_bass_kernel_spmd as _run

    nc = _bacc.Bacc("TRN2", target_bir_lowering=False, num_devices=1)
    arrays = {}

    def dram(name, a, dt=F32):
        arrays[name] = np.ascontiguousarray(a)
        return nc.dram_tensor(name, arrays[name].shape, dt, kind="ExternalInput").ap()

    ids = dram("ids", np.asarray(inputs["ids"]).reshape(BTILES, P, FIELDS).transpose(1, 0, 2), I32)
    tables = [dram(f"tbl_{f}", inputs[f"tbl_{f}"]) for f in range(FIELDS)]
    dense = dram("dense", inputs["dense_ctx"])
    w0 = dram("w0", np.asarray(inputs["L0_rec_W0"]).reshape(HID, FIELDS, FIELDS))
    w1 = dram("w1", np.asarray(inputs["L0_rec_W1"]).reshape(HID, FIELDS, HID))
    wt1 = dram("wt1", inputs["W_top1"])
    b1 = dram("b1", np.asarray(inputs["b_top1"]).reshape(TOP1 // P, P).T)
    wt2 = dram("wt2", inputs["W_top2"])
    b2 = dram("b2", np.asarray(inputs["b_top2"]).reshape(TOP2 // P, P).T)
    wt3 = dram("wt3", np.asarray(inputs["W_top3"]).reshape(TOP2 // P, P).T)
    out = nc.dram_tensor("y", (1, BATCH), F32, kind="ExternalOutput").ap()
    build(nc, ids, tables, dense, w0, w1, wt1, b1, wt2, b2, wt3, out)
    r = _run(nc, [arrays], core_ids=[0])
    return np.asarray(r.results[0]["y"]).reshape(BATCH, 1)
```

```python
from contextlib import ExitStack

import numpy as np

import concourse.bass as bass
from concourse import mybir

F32 = mybir.dt.float32
F32R = mybir.dt.float32r
I32 = mybir.dt.int32
U32 = mybir.dt.uint32
ALU = mybir.AluOpType
ACT = mybir.ActivationFunctionType

P = 128
BATCH = 512
FIELDS = 39
DIM = 16
HID = 128
DENSE = 16
TOP1 = 512
TOP2 = 256
BTILES = BATCH // P

BLOCKS = 3
ROWS = BLOCKS * FIELDS
PLAIN = (0, 3, 6, 9)
FANS = (9, 21)
TILES = ((0, 0, 3), (0, 1, 3), (0, 2, 3), (0, 3, 3), (1, 3, 3), (1, 2, 3), (1, 1, 2))
NT = len(TILES)


def covered_differences():
    out = []
    for fan, plain, blocks in TILES:
        for j in range(blocks):
            gap = (FANS[fan] + j - PLAIN[plain]) % FIELDS
            out.append(min(gap, FIELDS - gap))
    return sorted(out)


assert covered_differences() == list(range(FIELDS // 2 + 1))

CHUNK_D = 4
CHUNKS = DIM // CHUNK_D
COLS = CHUNK_D * P
STEPS = BTILES * CHUNKS
SLOTS = CHUNKS * NT
GROUP = P // DIM
GROUPS = P // GROUP
HALVES = 2
SHARE = GROUP // HALVES
HROWS = P // HALVES
BATCH_G = 4
BATCHES = GROUPS // BATCH_G
BANK_G = 2
SUBS = BATCH_G // BANK_G
XF = FIELDS + 1

SPLIT_OF = (2, 7, 7, 7)
W0_SPLIT = max(SPLIT_OF)
W0_WHOLE = min(SPLIT_OF)
SPLIT_PAIRS = [(s, pair) for s in range(STEPS) for pair in range((SPLIT_OF[s // CHUNKS] + 1) // 2)]
DIRECT_TILES = [(s, n) for s in range(STEPS) for n in range(SPLIT_OF[s // CHUNKS], NT)]
P_RING = 2
SPLIT_RING = 4
DIRECT_RING = 5

TURN_AT = 2
ROUND_AT = (1, 2, 4, 6)
EARLY = 4
ROWS_DVE = (0, 1, 3)
W1_FIRST = 4
W1_EARLY = 6


def late(t):
    return 2 if t == 1 else 0


def form_after(t, j):
    return {0: (0, 1), 1: (2, 3)}.get(j - late(t), ())


def round_after(t, j):
    return {1: (0,), 2: (1,)}.get(j - late(t), ())


def rest_after(t, j):
    return {2: (0,)}.get(j - late(t), ())


XT_SLOT = (17, 23)
Z2_SLOT = 0
Z2_FIRST = 7
Z2_EACH = 3
Z2_PARTS = ((0, Z2_FIRST),) + tuple((f, min(f + Z2_EACH, FIELDS)) for f in range(Z2_FIRST, FIELDS, Z2_EACH))
Z2_END = Z2_SLOT + len(Z2_PARTS) - 1
MLP1_SLOT = Z2_END + 3
MLP2_SLOT = MLP1_SLOT + 2
MLP3_SLOT = MLP2_SLOT + 3
assert (CHUNKS - 3) * NT + TURN_AT < MLP1_SLOT and MLP3_SLOT < SLOTS
WT_BANKS = (FIELDS + 3) // 4


def build(nc, ids, tables, dense, w0, w1, wt1, b1, wt2, b2, wt3, out):
    with ExitStack() as ctx:
        def sb(name, shape, dt=F32):
            return ctx.enter_context(nc.sbuf_tensor(name, shape, dt))

        def bank(name):
            return ctx.enter_context(nc.psum_tensor(name, [P, 512], F32))

        def sem(name):
            return ctx.enter_context(nc.semaphore(name))

        MADE = len(PLAIN) - 1 + len(FANS)

        idx = sb("idx", [P, BTILES, FIELDS], I32)
        x_rows = sb("x_rows", [P, 2, FIELDS * DIM])
        x_rep = sb("x_rep", [P, P, DIM])
        ident = sb("ident", [P, P])
        x_turned = sb("x_turned", [P, 2, COLS])
        stacks = sb("stacks", [P, 2 * MADE * COLS + P * DIM])
        pairs = sb("pairs", [P, P_RING, 2, COLS])
        direct = sb("direct", [P, DIRECT_RING, COLS])
        pairs_hi = sb("pairs_hi", [P, SPLIT_RING, 2, COLS], F32R)
        pairs_lo = sb("pairs_lo", [P, SPLIT_RING, 2, COLS], F32R)
        w0_hi = sb("w0_hi", [P, W0_SPLIT, P], F32R)
        w0_lo = sb("w0_lo", [P, W0_SPLIT, P], F32R)
        w0_direct = sb("w0_direct", [P, NT - W0_WHOLE, P])
        w1_t = sb("w1_t", [P, FIELDS, P])
        h1 = sb("h1", [P, P * DIM])
        h1_rows = sb("h1_rows", [P, BATCHES, BATCH_G, P])
        own = sb("own", [P, SHARE])
        x_diag = sb("x_diag", [P, GROUPS, SHARE, XF])
        gram = sb("gram", [P, XF, P])
        z2_sb = sb("z2_sb", [P, P])
        dense_sb = sb("dense_sb", [P, BTILES, DENSE])
        dense_t = sb("dense_t", [DENSE, BATCH])
        wt1_z = sb("wt1_z", [P, 2, TOP1])
        wt1_d = sb("wt1_d", [DENSE, TOP1])
        wt2_sb = sb("wt2_sb", [P, TOP1 // P, TOP2])
        wt3_sb = sb("wt3_sb", [P, TOP2 // P])
        b1_sb = sb("b1_sb", [P, TOP1 // P])
        b2_sb = sb("b2_sb", [P, TOP2 // P])
        hid1 = sb("hid1", [P, TOP1 // P, P])
        hid2 = sb("hid2", [P, TOP2 // P, P])
        y_sb = sb("y_sb", [1, BATCH])

        x_tile = stacks[0:FIELDS, 2 * MADE * COLS:]

        def made(i, s, rows):
            at = (s % 2 * MADE + i) * COLS
            return stacks[rows, at:at + COLS]

        def plain_stack(plain, s, rows):
            return made(plain - 1, s, rows) if plain else x_turned[rows, s % 2, :]

        def fan_stack(fan, s, rows):
            return made(len(PLAIN) - 1 + fan, s, rows)

        direct_space = direct[:].rearrange("p r n -> p (r n)")
        wsym = stacks[:, 0:4 * FIELDS * FIELDS].rearrange("p (f q) -> p f q", q=2 * FIELDS)
        w0_raw = h1[:, 0:FIELDS * FIELDS].rearrange("p (f q) -> p f q", q=FIELDS)
        w0_tiles = direct_space[:, 0:NT * ROWS].rearrange("p (n r) -> p n r", r=ROWS)
        w1_raw = gram[:].rearrange("p f q -> p (f q)")[:, 0:FIELDS * HID].rearrange(
            "p (f q) -> p f q", q=HID)

        T = bank("turn_bank")
        L = [bank("layer1_bank0"), bank("layer1_bank1")]
        M = bank("tower_bank")
        G = [bank(f"gram_bank{i}") for i in range(SUBS * HALVES)]

        ids_in = sem("ids_in")
        w0_in = sem("w0_in")
        w1_in = sem("w1_in")
        small_in = sem("small_in")
        x_landed = [sem(f"x_landed{t}") for t in range(BTILES)]
        ident_zero = sem("ident_zero")
        ident_done = sem("ident_done")
        sym_done = sem("sym_done")
        w0_tiled = sem("w0_tiled")
        own_done = sem("own_done")
        ones_done = sem("ones_done")
        w0_turned = sem("w0_turned")
        w0_hi_done = sem("w0_hi_done")
        w0_direct_done = sem("w0_direct_done")
        w0_lo_done = sem("w0_lo_done")
        w1_turned = sem("w1_turned")
        w1_kept_act = sem("w1_kept_act")
        w1_kept_dve = sem("w1_kept_dve")
        dense_turned = sem("dense_turned")
        dense_kept = sem("dense_kept")
        x_rep_done = sem("x_rep_done")
        x_turned_done = sem("x_turned_done")
        x_turned_kept = sem("x_turned_kept")
        x_tile_kept = sem("x_tile_kept")
        stack_in = [[sem(f"stack{i}_in{slot}") for i in range(MADE)] for slot in range(2)]
        split_formed = sem("split_formed")
        direct_formed = sem("direct_formed")
        hi_done = sem("hi_done")
        lo_done = sem("lo_done")
        tile_used = sem("tile_used")
        h1_kept = sem("h1_kept")
        xcols_turned = sem("xcols_turned")
        xdiag_kept = sem("xdiag_kept")
        rows_turned = sem("rows_turned")
        rows_kept_act = sem("rows_kept_act")
        rows_kept_dve = sem("rows_kept_dve")
        gram_done = sem("gram_done")
        gram_kept_act = sem("gram_kept_act")
        gram_kept_dve = sem("gram_kept_dve")
        z2_done = sem("z2_done")
        z2_kept = sem("z2_kept")
        top1_done = sem("top1_done")
        top1_kept = sem("top1_kept")
        top2_done = sem("top2_done")
        top2_kept = sem("top2_kept")
        y_done = sem("y_done")
        y_kept = sem("y_kept")
        y_out = sem("y_out")

        SMALL_LOADS = 7

        def tile_rows(n):
            return TILES[n][2] * FIELDS

        BANK_TILES = 4

        def w0_bank(n0, n1):
            first = n0 // BANK_TILES * BANK_TILES
            cols = L[n0 // BANK_TILES][0:tile_rows(n0), (n0 - first) * HID:(n1 - first) * HID]
            return cols.rearrange("p (n h) -> p n h", h=HID)

        W0_SPLIT_PARTS = (((0, BANK_TILES),), ((BANK_TILES, NT - 1), (NT - 1, W0_SPLIT)))
        W0_WHOLE_PARTS = (((W0_WHOLE, BANK_TILES),), ((BANK_TILES, NT - 1), (NT - 1, NT)))

        def w1_bank(n):
            return G[n % 4]

        def w1_count(n):
            return min(4, FIELDS - 4 * n)

        def kept_before(n, parity):
            return (n - parity) // 2 + 1

        def gram_bank(sub, half):
            return G[sub * HALVES + half][:, 0:BANK_G * SHARE * XF].rearrange("p (g b f) -> p g b f", b=SHARE, f=XF)

        z2_bank = G[0][:, 0:P]
        top1_banks = [G[1][:, 0:P], G[2][:, 0:P], G[3][:, 0:P], T[:, 0:P]]
        top2_banks = [G[0][:, 0:P], G[1][:, 0:P]]
        y_bank = G[2][0:1, 0:P]

        def rows_bank(j):
            return L[1] if j % 2 else M

        def rows_kept(u, j):
            mine = [i for i in range(BATCHES) if (i in ROWS_DVE) == (j in ROWS_DVE)]
            return rows_kept_dve if j in ROWS_DVE else rows_kept_act, len(mine) * u + mine.index(j) + 1

        def split_tiles(s):
            return SPLIT_OF[s // CHUNKS]

        def split_pairs(s):
            return (split_tiles(s) + 1) // 2

        def pairs_before(s):
            return sum(split_pairs(i) for i in range(s))

        def splits_before(s):
            return sum(split_tiles(i) for i in range(s))

        def pair_end(s, pair):
            return min(2 * pair + 2, split_tiles(s))

        def directs_before(s):
            return sum(NT - split_tiles(i) for i in range(s))

        def pair_slot(s, pair):
            return (pairs_before(s) + pair) % SPLIT_RING

        def direct_at(s, n):
            return directs_before(s) + n - split_tiles(s)

        def direct_slot(s, n):
            return direct_at(s, n) % DIRECT_RING

        def pair_used(at):
            s, pair = SPLIT_PAIRS[at]
            return NT * s + pair_end(s, pair)

        def direct_used(at):
            s, n = DIRECT_TILES[at]
            return NT * s + n + 1

        block = ctx.enter_context(nc.Block())

        @block.sync
        def _(sp):
            sp.dma_start(idx[:], ids).then_inc(ids_in, 16)
            sp.dma_start(w0_raw, w0).then_inc(w0_in, 16)
            sp.dma_start(w1_raw, w1).then_inc(w1_in, 16)
            sp.dma_start(dense_sb[:], dense.rearrange("(t p) c -> p t c", p=P)).then_inc(small_in, 16)
            sp.dma_start(wt1_z[:], wt1[0:2 * HID, :].rearrange("(k p) n -> p k n", p=P)).then_inc(small_in, 16)
            sp.dma_start(wt1_d[:], wt1[2 * HID:2 * HID + DENSE, :]).then_inc(small_in, 16)
            sp.dma_start(wt2_sb[:], wt2.rearrange("(k p) n -> p k n", p=P)).then_inc(small_in, 16)
            sp.dma_start(wt3_sb[:], wt3).then_inc(small_in, 16)
            sp.dma_start(b1_sb[:], b1).then_inc(small_in, 16)
            sp.dma_start(b2_sb[:], b2).then_inc(small_in, 16)

            def make_stacks(s):
                sp.wait_ge(x_turned_kept, s + 1)
                if s >= 2:
                    sp.wait_ge(split_formed, splits_before(s - 1))
                    sp.wait_ge(direct_formed, directs_before(s - 1))

                def make_fan(fan):
                    for j in range(BLOCKS):
                        first = FANS[fan] + j
                        sp.dma_start(fan_stack(fan, s, slice(j * FIELDS, (j + 1) * FIELDS)),
                                     x_turned[first:first + FIELDS, s % 2, :]
                                     ).then_inc(stack_in[s % 2][len(PLAIN) - 1 + fan], 16)

                make_fan(0)
                for plain in range(1, len(PLAIN)):
                    sp.dma_start(plain_stack(plain, s, slice(0, ROWS)),
                                 x_turned[PLAIN[plain]:PLAIN[plain] + ROWS, s % 2, :]
                                 ).then_inc(stack_in[s % 2][plain - 1], 16)
                make_fan(1)

            for s in range(STEPS):
                make_stacks(s)
            sp.wait_ge(y_kept, BTILES)
            sp.dma_start(out, y_sb[:]).then_inc(y_out, 16)
            sp.wait_ge(y_out, 16)

        @block.gpsimd
        def _(pool):
            nc.gpsimd.memset(ident[:], 0.0).then_inc(ident_zero, 1)
            pool.wait_ge(ident_zero, 1)
            nc.gpsimd.affine_select(out=ident[:], in_=ident[:], compare_op=ALU.not_equal, fill=1.0,
                                    base=0, pattern=[[-1, P]], channel_multiplier=1).then_inc(ident_done, 1)
            pool.wait_ge(ids_in, 16)
            for t in range(BTILES):
                if t >= 2:
                    pool.wait_ge(x_rep_done, 2 * (t - 1))
                for f in range(FIELDS):
                    nc.gpsimd.indirect_dma_start(
                        out=x_rows[:, t % 2, f * DIM:(f + 1) * DIM], out_offset=None, in_=tables[f],
                        in_offset=bass.IndirectOffsetOnAxis(ap=idx[:, t, f:f + 1].bitcast(U32), axis=0),
                    ).then_inc(x_landed[t], 16)

        @block.scalar
        def _(act):
            for i in range(2):
                act.wait_ge(w0_turned, i + 1)
                for n0, n1 in W0_SPLIT_PARTS[i]:
                    nc.scalar.activation(w0_hi[0:tile_rows(n0), n0:n1, :], w0_bank(n0, n1),
                                         ACT.Copy).then_inc(w0_hi_done, 1)
                for n0, n1 in W0_WHOLE_PARTS[i]:
                    nc.scalar.activation(w0_direct[0:tile_rows(n0), n0 - W0_WHOLE:n1 - W0_WHOLE, :],
                                         w0_bank(n0, n1), ACT.Copy).then_inc(w0_direct_done, 1)
            def keep_turned(s):
                t, c = divmod(s, CHUNKS)
                act.wait_ge(x_turned_done, s + 1)
                if s >= 2:
                    act.wait_ge(split_formed, splits_before(s - 1))
                    act.wait_ge(direct_formed, directs_before(s - 1))
                nc.scalar.activation(x_turned[:, s % 2, :], T[:], ACT.Copy).then_inc(x_turned_kept, 1)
                if t and c == 0:
                    act.wait_ge(xcols_turned, 2 * t)
                dst = x_tile.rearrange("p (b d) -> p d b", d=DIM)[:, c * CHUNK_D:(c + 1) * CHUNK_D, :]
                nc.scalar.activation(dst, T[0:FIELDS, :].rearrange("p (d b) -> p d b", b=P),
                                     ACT.Copy).then_inc(x_tile_kept, 1)

            def keep_h1(s):
                t, c = divmod(s, CHUNKS)
                act.wait_ge(tile_used, NT * (s + 1))
                if t and c == 0:
                    act.wait_ge(rows_turned, BATCHES * t)
                dst = h1[:].rearrange("p (b d) -> p d b", d=DIM)[:, c * CHUNK_D:(c + 1) * CHUNK_D, :]
                nc.scalar.activation(dst, L[s % 2][:].rearrange("p (d b) -> p d b", b=P),
                                     ACT.Copy).then_inc(h1_kept, 1)

            def round_pairs(s, pair):
                at = pairs_before(s) + pair
                end = pair_end(s, pair)
                rows, count = tile_rows(end - 1), end - 2 * pair
                act.wait_ge(split_formed, splits_before(s) + end)
                if at >= SPLIT_RING:
                    act.wait_ge(tile_used, pair_used(at - SPLIT_RING))
                nc.scalar.activation(pairs_hi[0:rows, pair_slot(s, pair), 0:count, :],
                                     pairs[0:rows, at % P_RING, 0:count, :],
                                     ACT.Copy).then_inc(hi_done, 1)

            def keep_xdiag(u, half):
                g0 = half * GROUPS // 2
                act.wait_ge(xcols_turned, 2 * u + half + 1)
                if u == 0:
                    act.wait_ge(own_done, 1)
                else:
                    act.wait_ge(gram_done, SUBS * BATCHES * u)
                for b in range(SHARE):
                    nc.scalar.activation(
                        x_diag[:, g0:g0 + GROUPS // 2, b, 0:FIELDS],
                        M[:, 0:GROUPS // 2 * FIELDS].rearrange("p (g f) -> p g f", f=FIELDS),
                        ACT.Copy, scale=own[:, b:b + 1]).then_inc(xdiag_kept, 1)

            def keep_rows(u, j):
                act.wait_ge(rows_turned, BATCHES * u + j + 1)
                if u:
                    act.wait_ge(gram_done, SUBS * (BATCHES * (u - 1) + j + 1))
                nc.scalar.activation(h1_rows[:, j, :, :], rows_bank(j)[:].rearrange("p (g q) -> p g q", q=HID),
                                     ACT.Copy).then_inc(rows_kept_act, 1)

            def keep_gram(u, j):
                if u and j == 0:
                    act.wait_ge(top1_done, TOP1 // P * u)
                to = gram[:].rearrange("p f (g i b) -> p g i b f", i=HALVES, b=SHARE)
                for sub in range(SUBS):
                    g0 = j * BATCH_G + sub * BANK_G
                    act.wait_ge(gram_done, SUBS * (BATCHES * u + j) + sub + 1)
                    nc.scalar.activation(to[:, g0:g0 + BANK_G, 0, :, :], gram_bank(sub, 0),
                                         ACT.Copy).then_inc(gram_kept_act, 1)

            def tower(u, k):
                if k == Z2_END:
                    act.wait_ge(z2_done, u + 1)
                    if u:
                        act.wait_ge(top1_done, TOP1 // P * u)
                    nc.scalar.activation(z2_sb[:], z2_bank, ACT.Copy).then_inc(z2_kept, 1)
                if k == MLP1_SLOT:
                    if u == 0:
                        act.wait_ge(small_in, 16 * SMALL_LOADS)
                    else:
                        act.wait_ge(top2_done, TOP2 // P * u)
                    for m in range(TOP1 // P):
                        act.wait_ge(top1_done, TOP1 // P * u + m + 1)
                        nc.scalar.activation(hid1[:, m, :], top1_banks[m], ACT.Relu,
                                             bias=b1_sb[:, m:m + 1]).then_inc(top1_kept, 1)
                if k == MLP2_SLOT:
                    if u:
                        act.wait_ge(y_done, u)
                    for m in range(TOP2 // P):
                        act.wait_ge(top2_done, TOP2 // P * u + m + 1)
                        nc.scalar.activation(hid2[:, m, :], top2_banks[m], ACT.Relu,
                                             bias=b2_sb[:, m:m + 1]).then_inc(top2_kept, 1)
                if k == MLP3_SLOT:
                    act.wait_ge(y_done, u + 1)
                    nc.scalar.activation(y_sb[0:1, u * P:(u + 1) * P], y_bank, ACT.Copy).then_inc(y_kept, 1)

            def gram_stage(u, t):
                keep_h1(CHUNKS * (u + 1) - 1)
                if 1 < t < BTILES:
                    keep_turned(CHUNKS * t)
                for j in range(BATCHES):
                    if j not in ROWS_DVE:
                        keep_rows(u, j)
                if 1 < t < BTILES:
                    keep_turned(CHUNKS * t + 1)
                for j in range(BATCHES):
                    keep_gram(u, j)
                    if t == 1 and j < 2:
                        keep_turned(CHUNKS * t + j)
                    if t < BTILES:
                        for pair in round_after(t, j):
                            round_pairs(CHUNKS * t, pair)
                if t < BTILES:
                    rounded = [pair for j in range(BATCHES) for pair in round_after(t, j)]
                    for pair in range(len(rounded), split_pairs(CHUNKS * t)):
                        round_pairs(CHUNKS * t, pair)

            def keep_w1(n):
                act.wait_ge(w1_turned, n + 1)
                nc.scalar.activation(w1_t[:, 4 * n:4 * n + w1_count(n), :],
                                     w1_bank(n)[:, 0:w1_count(n) * HID].rearrange("p (n h) -> p n h", h=HID),
                                     ACT.Copy).then_inc(w1_kept_act, 1)

            def keep_w1_banks(n0, n1):
                for n in range(n0, n1):
                    if n % 2 == 0:
                        keep_w1(n)

            keep_w1_banks(0, W1_FIRST)
            act.wait_ge(dense_turned, 1)
            nc.scalar.activation(dense_t[:], M[0:DENSE, :], ACT.Copy).then_inc(dense_kept, 1)
            keep_turned(0)
            keep_w1_banks(W1_FIRST, W1_EARLY)
            keep_turned(1)
            keep_w1_banks(W1_EARLY, WT_BANKS)
            for t in range(BTILES):
                if t:
                    gram_stage(t - 1, t)
                else:
                    for pair in range(split_pairs(0)):
                        round_pairs(0, pair)
                for c in range(CHUNKS):
                    s = CHUNKS * t + c
                    for n in range(NT):
                        if n == 0 and c:
                            keep_h1(s - 1)
                        if t:
                            tower(t - 1, c * NT + n)
                        if n in ROUND_AT[0:split_pairs(s)] and c + 1 < CHUNKS:
                            round_pairs(s + 1, ROUND_AT.index(n))
                        if n == TURN_AT and c + 2 < CHUNKS:
                            keep_turned(s + 2)
                        if c * NT + n in XT_SLOT:
                            keep_xdiag(t, XT_SLOT.index(c * NT + n))
            gram_stage(BTILES - 1, BTILES)
            for k in (Z2_END, MLP1_SLOT, MLP2_SLOT, MLP3_SLOT):
                tower(BTILES - 1, k)

        @block.vector
        def _(dve):
            dve.wait_ge(ident_done, 1)
            nc.vector.tensor_reduce(own[:], ident[:].rearrange("p (i b d) -> p b i d", b=SHARE, d=DIM),
                                    mybir.AxisListType.XY, ALU.add).then_inc(own_done, 1)
            dve.wait_ge(own_done, 1)
            for b in range(SHARE):
                nc.vector.tensor_copy(x_diag[:, :, b, FIELDS], own[:, b:b + 1].to_broadcast([P, GROUPS])
                                      ).then_inc(ones_done, 1)
            dve.wait_ge(w0_in, 16)
            corner = wsym[:, 0:FIELDS, 0:FIELDS]
            nc.vector.tensor_tensor(corner, w0_raw, w0_raw.rearrange("p f q -> p q f"), ALU.add).then_inc(sym_done, 1)
            dve.wait_ge(sym_done, 1)
            diagonal = bass.AP(tensor=corner.tensor, offset=corner.offset,
                               ap=[list(corner.ap[0]), [2 * FIELDS + 1, FIELDS]])
            nc.vector.tensor_scalar(diagonal, diagonal, 0.5, None, ALU.mult).then_inc(sym_done, 1)
            dve.wait_ge(sym_done, 2)
            nc.vector.tensor_copy(wsym[:, 0:FIELDS, FIELDS:2 * FIELDS], corner).then_inc(sym_done, 1)
            dve.wait_ge(sym_done, 3)
            nc.vector.tensor_copy(wsym[:, FIELDS:2 * FIELDS, :], wsym[:, 0:FIELDS, :]).then_inc(sym_done, 1)
            for n, (fan, plain, blocks) in enumerate(TILES):
                dve.wait_ge(sym_done, 4)
                at = wsym[:, FANS[fan], PLAIN[plain]:PLAIN[plain] + 1]
                rows = bass.AP(tensor=at.tensor, offset=at.offset,
                               ap=[list(at.ap[0]), [2 * FIELDS, blocks], [2 * FIELDS + 1, FIELDS]])
                nc.vector.tensor_copy(w0_tiles[:, n, 0:blocks * FIELDS].rearrange("p (j f) -> p j f", j=blocks),
                                      rows).then_inc(w0_tiled, 1)
            for i in range(2):
                dve.wait_ge(w0_hi_done, sum(len(parts) for parts in W0_SPLIT_PARTS[0:i + 1]))
                dve.wait_ge(w0_direct_done, sum(len(parts) for parts in W0_WHOLE_PARTS[0:i + 1]))
                for n0, n1 in W0_SPLIT_PARTS[i]:
                    rows = tile_rows(n0)
                    nc.vector.tensor_tensor(w0_lo[0:rows, n0:n1, :], w0_bank(n0, n1),
                                            w0_hi[0:rows, n0:n1, :].bitcast(F32), ALU.subtract
                                            ).then_inc(w0_lo_done, 1)
            def repeat_fields(t):
                dve.wait_ge(x_landed[t], 16 * FIELDS)
                if t:
                    dve.wait_ge(x_turned_done, CHUNKS * t)
                whole = P // FIELDS
                nc.vector.tensor_copy(x_rep[:, 0:whole * FIELDS, :].rearrange("p (r f) d -> p r (f d)", r=whole),
                                      x_rows[:, t % 2:t % 2 + 1, :].to_broadcast([P, whole, FIELDS * DIM])
                                      ).then_inc(x_rep_done, 1)
                nc.vector.tensor_copy(x_rep[:, whole * FIELDS:, :].rearrange("p f d -> p (f d)"),
                                      x_rows[:, t % 2, 0:(P - whole * FIELDS) * DIM]).then_inc(x_rep_done, 1)

            def form_pairs(s, n):
                fan, plain, blocks = TILES[n]
                rows = blocks * FIELDS
                uses = s // 2 + 1
                dve.wait_ge(stack_in[s % 2][len(PLAIN) - 1 + fan], 16 * BLOCKS * uses)
                if plain:
                    dve.wait_ge(stack_in[s % 2][plain - 1], 16 * uses)
                if n < split_tiles(s):
                    at = pairs_before(s) + n // 2
                    if at >= P_RING:
                        dve.wait_ge(hi_done, at - P_RING + 1)
                        dve.wait_ge(lo_done, at - P_RING + 1)
                    to = pairs[0:rows, at % P_RING, n % 2, :]
                else:
                    at = direct_at(s, n)
                    if at >= DIRECT_RING:
                        dve.wait_ge(tile_used, direct_used(at - DIRECT_RING))
                    to = direct[0:rows, direct_slot(s, n), :]
                nc.vector.tensor_tensor(to, plain_stack(plain, s, slice(0, rows)), fan_stack(fan, s, slice(0, rows)),
                                        ALU.mult).then_inc(split_formed if n < split_tiles(s) else direct_formed, 1)

            def rest_pairs(s, pair):
                at = pairs_before(s) + pair
                end = pair_end(s, pair)
                rows, count = tile_rows(end - 1), end - 2 * pair
                slot = pair_slot(s, pair)
                dve.wait_ge(hi_done, at + 1)
                nc.vector.tensor_tensor(pairs_lo[0:rows, slot, 0:count, :], pairs[0:rows, at % P_RING, 0:count, :],
                                        pairs_hi[0:rows, slot, 0:count, :].bitcast(F32), ALU.subtract).then_inc(lo_done, 1)

            def keep_rows(u, j):
                dve.wait_ge(rows_turned, BATCHES * u + j + 1)
                if u:
                    dve.wait_ge(gram_done, SUBS * (BATCHES * (u - 1) + j + 1))
                nc.vector.tensor_copy(h1_rows[:, j, :, :], rows_bank(j)[:].rearrange("p (g q) -> p g q", q=HID)
                                      ).then_inc(rows_kept_dve, 1)

            def keep_gram(u, j):
                if u and j == 0:
                    dve.wait_ge(top1_done, TOP1 // P * u)
                to = gram[:].rearrange("p f (g i b) -> p g i b f", i=HALVES, b=SHARE)
                for sub in range(SUBS):
                    g0 = j * BATCH_G + sub * BANK_G
                    dve.wait_ge(gram_done, SUBS * (BATCHES * u + j) + sub + 1)
                    nc.vector.tensor_copy(to[:, g0:g0 + BANK_G, 1, :, :], gram_bank(sub, 1)
                                          ).then_inc(gram_kept_dve, 1)

            def form_chunk(s, first):
                for n in range(first, NT):
                    form_pairs(s, n)
                    if n % 2 and n > 2 and n // 2 - 1 < split_pairs(s):
                        rest_pairs(s, n // 2 - 1)
                for pair in range(NT // 2 - 1, split_pairs(s)):
                    rest_pairs(s, pair)

            def gram_stage(u, t):
                for j in ROWS_DVE:
                    keep_rows(u, j)
                if t == 1:
                    repeat_fields(1)
                for j in range(BATCHES):
                    keep_gram(u, j)
                    if t < BTILES:
                        for n in form_after(t, j):
                            form_pairs(CHUNKS * t, n)
                        for pair in rest_after(t, j):
                            rest_pairs(CHUNKS * t, pair)
                if t < BTILES and BATCHES <= 2 + late(t):
                    rest_pairs(CHUNKS * t, 0)

            def keep_w1_banks(n0, n1):
                for n in range(n0, n1):
                    if n % 2:
                        dve.wait_ge(w1_turned, n + 1)
                        nc.vector.tensor_copy(w1_t[:, 4 * n:4 * n + w1_count(n), :],
                                              w1_bank(n)[:, 0:w1_count(n) * HID].rearrange("p (n h) -> p n h", h=HID)
                                              ).then_inc(w1_kept_dve, 1)

            keep_w1_banks(0, W1_FIRST)
            repeat_fields(0)
            keep_w1_banks(W1_FIRST, WT_BANKS)
            for t in range(BTILES):
                if t:
                    gram_stage(t - 1, t)
                for c in range(CHUNKS):
                    form_chunk(CHUNKS * t + c, EARLY if t and c == 0 else 0)
                if 0 < t < BTILES - 1:
                    repeat_fields(t + 1)
            gram_stage(BTILES - 1, BTILES)

        @block.tensor
        def _(pe):
            pe.wait_ge(ident_done, 1)
            pe.wait_ge(w0_tiled, NT)
            for n, (fan, plain, blocks) in enumerate(TILES):
                at = n % BANK_TILES
                last = nc.tensor.transpose(L[n // BANK_TILES][0:blocks * FIELDS, at * P:(at + 1) * P],
                                           w0_tiles[:, n, 0:blocks * FIELDS], ident[:])
                if n in (BANK_TILES - 1, NT - 1):
                    last.then_inc(w0_turned, 1)
            def turn_w1(n):
                if n == 0:
                    pe.wait_ge(w1_in, 16)
                if n >= 4:
                    pe.wait_ge(w1_kept_dve if n % 2 else w1_kept_act, kept_before(n - 4, n % 2))
                for j in range(w1_count(n)):
                    last = nc.tensor.transpose(w1_bank(n)[:, j * P:(j + 1) * P], w1_raw[:, 4 * n + j, :], ident[:])
                last.then_inc(w1_turned, 1)

            def turn_x(s):
                t, c = divmod(s, CHUNKS)
                if s:
                    pe.wait_ge(x_tile_kept, s)
                if c == 0:
                    pe.wait_ge(x_rep_done, 2 * (t + 1))
                for j in range(CHUNK_D):
                    last = nc.tensor.transpose(T[:, j * P:(j + 1) * P], x_rep[:, :, c * CHUNK_D + j], ident[:])
                last.then_inc(x_turned_done, 1)

            def layer1(s, n):
                rows = TILES[n][2] * FIELDS
                if s == 0 and n == 0:
                    pe.wait_ge(w0_lo_done, sum(len(parts) for parts in W0_SPLIT_PARTS))
                if n == 0 and s >= 2:
                    pe.wait_ge(h1_kept, s - 1)
                if n == 0 and s >= CHUNKS and s % CHUNKS == 1:
                    pe.wait_ge(*rows_kept(s // CHUNKS - 1, BATCHES - 1))
                acc = L[s % 2][:]
                if n < split_tiles(s):
                    slot = pair_slot(s, n // 2)
                    if n % 2 == 0:
                        pe.wait_ge(lo_done, pairs_before(s) + n // 2 + 1)
                    hi, lo = pairs_hi[0:rows, slot, n % 2, :], pairs_lo[0:rows, slot, n % 2, :]
                    nc.tensor.matmul(acc, w0_hi[0:rows, n, :], hi, start=(n == 0), stop=False)
                    nc.tensor.matmul(acc, w0_hi[0:rows, n, :], lo, start=False, stop=False)
                    last = nc.tensor.matmul(acc, w0_lo[0:rows, n, :], hi, start=False, stop=(n == NT - 1))
                else:
                    pe.wait_ge(direct_formed, direct_at(s, n) + 1)
                    last = nc.tensor.matmul(acc, w0_direct[0:rows, n - W0_WHOLE, :], direct[0:rows, direct_slot(s, n), :],
                                            start=(n == 0), stop=(n == NT - 1))
                last.then_inc(tile_used, 1)

            def turn_xcols(u, half):
                pe.wait_ge(x_tile_kept, CHUNKS * (u + 1))
                if half:
                    pe.wait_ge(xdiag_kept, SHARE * (2 * u + 1))
                elif u == 0:
                    pe.wait_ge(dense_kept, 1)
                for g in range(GROUPS // 2):
                    at = (half * GROUPS // 2 + g) * P
                    last = nc.tensor.transpose(M[:, g * FIELDS:(g + 1) * FIELDS], x_tile[:, at:at + P],
                                               ident[0:FIELDS, 0:FIELDS])
                last.then_inc(xcols_turned, 1)

            def turn_h1(u, j):
                if j == 0:
                    pe.wait_ge(h1_kept, CHUNKS * (u + 1))
                if j:
                    if j >= 2:
                        pe.wait_ge(*rows_kept(u, j - 2))
                else:
                    pe.wait_ge(xdiag_kept, SHARE * 2 * (u + 1))
                for g in range(BATCH_G):
                    at = (BATCH_G * j + g) * P
                    last = nc.tensor.transpose(rows_bank(j)[:, g * P:(g + 1) * P], h1[:, at:at + P], ident[:])
                last.then_inc(rows_turned, 1)

            def form_gram(u, j):
                if u == 0 and j == 0:
                    pe.wait_ge(ones_done, SHARE)
                    pe.wait_ge(w1_kept_act, (WT_BANKS + 1) // 2)
                    pe.wait_ge(w1_kept_dve, WT_BANKS // 2)
                pe.wait_ge(*rows_kept(u, j))
                if u and j == 0:
                    pe.wait_ge(y_kept, u)
                for sub in range(SUBS):
                    at = SUBS * (BATCHES * u + j) + sub
                    if at >= SUBS:
                        pe.wait_ge(gram_kept_act, at - SUBS + 1)
                        pe.wait_ge(gram_kept_dve, at - SUBS + 1)
                    for b in range(BANK_G):
                        g = sub * BANK_G + b
                        for i in range(HALVES):
                            rows = slice(i * HROWS, (i + 1) * HROWS)
                            last = nc.tensor.matmul(
                                G[sub * HALVES + i][:, b * SHARE * XF:(b + 1) * SHARE * XF],
                                h1_rows[rows, j, g, :], x_diag[rows, BATCH_G * j + g, :, :],
                                start=True, stop=True)
                    last.then_inc(gram_done, 1)

            def gram_stage(u, t):
                if 1 < t < BTILES:
                    turn_x(CHUNKS * t)
                turn_h1(u, 0)
                turn_h1(u, 1)
                turn_h1(u, 2)
                if 1 < t < BTILES:
                    turn_x(CHUNKS * t + 1)
                turn_h1(u, 3)
                for j in range(BATCHES):
                    form_gram(u, j)
                    if t == 1 and j < 2:
                        turn_x(CHUNKS * t + j)

            def tower(u, k):
                if Z2_SLOT <= k <= Z2_END:
                    f0, f1 = Z2_PARTS[k - Z2_SLOT]
                    if f0 == 0:
                        pe.wait_ge(gram_kept_act, SUBS * BATCHES * (u + 1))
                        pe.wait_ge(gram_kept_dve, SUBS * BATCHES * (u + 1))
                    for f in range(f0, f1):
                        last = nc.tensor.matmul(z2_bank, w1_t[:, f, :], gram[:, f, :],
                                                start=(f == 0), stop=(f == FIELDS - 1))
                    if f1 == FIELDS:
                        last.then_inc(z2_done, 1)
                if k == MLP1_SLOT:
                    pe.wait_ge(x_tile_kept, CHUNKS * min(u + 2, BTILES))
                    for m in range(TOP1 // P):
                        cols = slice(m * P, (m + 1) * P)
                        nc.tensor.matmul(top1_banks[m], wt1_d[:, cols], dense_t[:, u * P:(u + 1) * P],
                                         start=True, stop=False)
                        nc.tensor.matmul(top1_banks[m], wt1_z[:, 0, cols], gram[:, FIELDS, :],
                                         start=False, stop=False)
                    pe.wait_ge(z2_kept, u + 1)
                    for m in range(TOP1 // P):
                        last = nc.tensor.matmul(top1_banks[m], wt1_z[:, 1, m * P:(m + 1) * P], z2_sb[:],
                                                start=False, stop=True)
                        last.then_inc(top1_done, 1)
                if k == MLP2_SLOT:
                    for j in range(TOP1 // P):
                        pe.wait_ge(top1_kept, TOP1 // P * u + j + 1)
                        for m in range(TOP2 // P):
                            last = nc.tensor.matmul(top2_banks[m], wt2_sb[:, j, m * P:(m + 1) * P], hid1[:, j, :],
                                                    start=(j == 0), stop=(j == TOP1 // P - 1))
                            if j == TOP1 // P - 1:
                                last.then_inc(top2_done, 1)
                if k == MLP3_SLOT:
                    for j in range(TOP2 // P):
                        pe.wait_ge(top2_kept, TOP2 // P * u + j + 1)
                        last = nc.tensor.matmul(y_bank, wt3_sb[:, j:j + 1], hid2[:, j, :],
                                                start=(j == 0), stop=(j == TOP2 // P - 1))
                    last.then_inc(y_done, 1)

            for n in range(W1_FIRST):
                turn_w1(n)
            pe.wait_ge(small_in, 16 * SMALL_LOADS)
            for t in range(BTILES):
                last = nc.tensor.transpose(M[0:DENSE, t * P:(t + 1) * P], dense_sb[:, t, :], ident[:])
            last.then_inc(dense_turned, 1)
            turn_x(0)
            for n in range(W1_FIRST, W1_EARLY):
                turn_w1(n)
            turn_x(1)
            for n in range(W1_EARLY, WT_BANKS):
                turn_w1(n)
            for t in range(BTILES):
                if t:
                    gram_stage(t - 1, t)
                for c in range(CHUNKS):
                    s = CHUNKS * t + c
                    for n in range(NT):
                        if t == 1:
                            tower(t - 1, c * NT + n)
                        layer1(s, n)
                        if t > 1:
                            tower(t - 1, c * NT + n)
                        if n == TURN_AT and c + 2 < CHUNKS:
                            turn_x(s + 2)
                        if c * NT + n in XT_SLOT:
                            turn_xcols(t, XT_SLOT.index(c * NT + n))
            gram_stage(BTILES - 1, BTILES)
            for k in range(Z2_SLOT, MLP3_SLOT + 1):
                tower(BTILES - 1, k)


def kernel(**inputs):
    import concourse.bacc as _bacc
    from concourse.bass_utils import run_bass_kernel_spmd as _run

    nc = _bacc.Bacc("TRN2", target_bir_lowering=False, num_devices=1)
    arrays = {}

    def dram(name, a, dt=F32):
        arrays[name] = np.ascontiguousarray(a)
        return nc.dram_tensor(name, arrays[name].shape, dt, kind="ExternalInput").ap()

    ids = dram("ids", np.asarray(inputs["ids"]).reshape(BTILES, P, FIELDS).transpose(1, 0, 2), I32)
    tables = [dram(f"tbl_{f}", inputs[f"tbl_{f}"]) for f in range(FIELDS)]
    dense = dram("dense", inputs["dense_ctx"])
    w0 = dram("w0", np.asarray(inputs["L0_rec_W0"]).reshape(HID, FIELDS, FIELDS))
    w1 = dram("w1", np.asarray(inputs["L0_rec_W1"]).reshape(HID, FIELDS, HID))
    wt1 = dram("wt1", inputs["W_top1"])
    b1 = dram("b1", np.asarray(inputs["b_top1"]).reshape(TOP1 // P, P).T)
    wt2 = dram("wt2", inputs["W_top2"])
    b2 = dram("b2", np.asarray(inputs["b_top2"]).reshape(TOP2 // P, P).T)
    wt3 = dram("wt3", np.asarray(inputs["W_top3"]).reshape(TOP2 // P, P).T)
    out = nc.dram_tensor("y", (1, BATCH), F32, kind="ExternalOutput").ap()
    build(nc, ids, tables, dense, w0, w1, wt1, b1, wt2, b2, wt3, out)
    r = _run(nc, [arrays], core_ids=[0])
    return np.asarray(r.results[0]["y"]).reshape(BATCH, 1)
```
